# Optimizing a Trainium2 kernel written in Bass

```python
import numpy as np
import jax
import jax.numpy as jnp

def _softmax(x, axis=-1):
    return jax.nn.softmax(x, axis=axis)

def _gelu(x):
    return jax.nn.gelu(x, approximate=True)

def _silu(x):
    return jax.nn.silu(x)

def _sigmoid(x):
    return jax.nn.sigmoid(x)

def _layernorm(x, axis=-1, eps=1e-05):
    m = jnp.mean(x, axis=axis, keepdims=True)
    v = jnp.var(x, axis=axis, keepdims=True)
    return (x - m) / jnp.sqrt(v + eps)

def _scatter_add(tgt, idx, src, axis=0):
    return tgt.at[idx].add(src)

def _segment_sum(src, seg, n):
    return jax.ops.segment_sum(src, seg, n)
kernel_name = 'mk_adaln_d1_jaxref_r4_6ecfae'

def setup_inputs(seed: int=0):
    np.random.seed(seed)
    _w = jnp.asarray

    def _L0_attn_setup():
        import jax, jax.numpy as jnp
        import numpy as np
        D_MODEL = 512
        NUM_HEADS = 16
        THETA = 10000.0

        def _rope(t, cos, sin):
            x_even = t[..., 0::2]
            x_odd = t[..., 1::2]
            rot = jnp.stack((-x_odd, x_even), axis=-1).reshape(t.shape)
            return t * cos + rot * sin
        key = jax.random.key(seed)
        ks = jax.random.split(key, 5)
        bs, S, d = (4, 512, D_MODEL)
        std = (2.0 / (d + d)) ** 0.5
        x = jax.random.normal(ks[0], (bs, S, d), dtype=jnp.float32)
        wq = jax.random.normal(ks[1], (d, d), dtype=jnp.float32) * std
        wk = jax.random.normal(ks[2], (d, d), dtype=jnp.float32) * std
        wv = jax.random.normal(ks[3], (d, d), dtype=jnp.float32) * std
        wo = jax.random.normal(ks[4], (d, d), dtype=jnp.float32) * std
        return {'x': x, 'wq': wq, 'wk': wk, 'wv': wv, 'wo': wo}
    _L0_attn_in = _L0_attn_setup()

    def _L0_ffn_setup():
        import jax, jax.numpy as jnp
        import numpy as np
        DIM_IN = 512
        DIM_HIDDEN = 2048
        key = jax.random.key(seed)
        k_x, k_g, k_u, k_d = jax.random.split(key, 4)
        s_in = 1.0 / np.sqrt(DIM_IN)
        s_hid = 1.0 / np.sqrt(DIM_HIDDEN)
        x = jax.random.normal(k_x, (4, 512, DIM_IN), dtype=jnp.float32)
        w_gate = jax.random.uniform(k_g, (DIM_HIDDEN, DIM_IN), jnp.float32, -s_in, s_in)
        w_up = jax.random.uniform(k_u, (DIM_HIDDEN, DIM_IN), jnp.float32, -s_in, s_in)
        w_down = jax.random.uniform(k_d, (DIM_IN, DIM_HIDDEN), jnp.float32, -s_hid, s_hid)
        return {'x': x, 'w_gate': w_gate, 'w_up': w_up, 'w_down': w_down}
    _L0_ffn_in = _L0_ffn_setup()
    _L0_c = _w((lambda *s: np.random.randn(*s).astype(np.float32) * 0.05)(2, 512))
    _L0_wmod = _w((lambda *s: np.random.randn(*s).astype(np.float32) * 0.05)(512, 6 * 512) * 512 ** (-0.5))
    _d = {'L0_attn_x': _L0_attn_in['x'], 'L0_attn_wq': _L0_attn_in['wq'], 'L0_attn_wk': _L0_attn_in['wk'], 'L0_attn_wv': _L0_attn_in['wv'], 'L0_attn_wo': _L0_attn_in['wo'], 'L0_ffn_w_gate': _L0_ffn_in['w_gate'], 'L0_ffn_w_up': _L0_ffn_in['w_up'], 'L0_ffn_w_down': _L0_ffn_in['w_down'], 'L0_c': _L0_c, 'L0_wmod': _L0_wmod}
    _x0 = _d['L0_attn_x']
    _d['L0_attn_x'] = jax.random.normal(jax.random.fold_in(jax.random.key(seed), 1), (2, 1024, 512), dtype=_x0.dtype)
    del _x0
    return _d

def reference(L0_attn_x, L0_attn_wq, L0_attn_wk, L0_attn_wv, L0_attn_wo, L0_ffn_w_gate, L0_ffn_w_up, L0_ffn_w_down, L0_c, L0_wmod):

    def _L0_attn_ref(x, wq, wk, wv, wo):
        import jax, jax.numpy as jnp
        import numpy as np
        D_MODEL = 512
        NUM_HEADS = 16
        THETA = 10000.0

        def _rope(t, cos, sin):
            x_even = t[..., 0::2]
            x_odd = t[..., 1::2]
            rot = jnp.stack((-x_odd, x_even), axis=-1).reshape(t.shape)
            return t * cos + rot * sin
        bs, S, d = x.shape
        H = NUM_HEADS
        dk = d // H
        q = (x @ wq.T).reshape(bs, S, H, dk).transpose(0, 2, 1, 3)
        k = (x @ wk.T).reshape(bs, S, H, dk).transpose(0, 2, 1, 3)
        v = (x @ wv.T).reshape(bs, S, H, dk).transpose(0, 2, 1, 3)
        half = dk // 2
        inv_freq = THETA ** (-2.0 * jnp.arange(half, dtype=jnp.float32) / dk)
        pos = jnp.arange(S, dtype=jnp.float32)
        ang = pos[:, None] * inv_freq[None, :]
        cos = jnp.repeat(jnp.cos(ang), 2, axis=-1)
        sin = jnp.repeat(jnp.sin(ang), 2, axis=-1)
        q = _rope(q, cos, sin)
        k = _rope(k, cos, sin)
        scale = 1.0 / jnp.sqrt(jnp.asarray(dk, dtype=x.dtype))
        attn = jnp.einsum('bhqd,bhkd->bhqk', q, k) * scale
        causal = jnp.tril(jnp.ones((S, S), dtype=bool))
        attn = jnp.where(causal, attn, -jnp.inf)
        probs = jax.nn.softmax(attn, axis=-1)
        out = jnp.einsum('bhqk,bhkd->bhqd', probs, v)
        out = out.transpose(0, 2, 1, 3).reshape(bs, S, d)
        return out @ wo.T

    def _L0_ffn_ref(x, w_gate, w_up, w_down):
        import jax, jax.numpy as jnp
        import numpy as np
        DIM_IN = 512
        DIM_HIDDEN = 2048
        gate = jnp.einsum('bsd,hd->bsh', x, w_gate)
        up = jnp.einsum('bsd,hd->bsh', x, w_up)
        gated = jax.nn.silu(gate) * up
        return jnp.einsum('bsh,dh->bsd', gated, w_down)
    x = L0_attn_x
    mod = (_silu(L0_c) @ L0_wmod).reshape(L0_c.shape[0], 6, 1, -1)
    sa, ca, ga, sb, cb, gb = (mod[:, 0], mod[:, 1], mod[:, 2], mod[:, 3], mod[:, 4], mod[:, 5])
    ga = (2 * (ga >= 0) - 1) * jnp.maximum(jnp.abs(ga), 0.25)
    gb = (2 * (gb >= 0) - 1) * jnp.maximum(jnp.abs(gb), 0.25)
    h = _layernorm(x, axis=-1) * (1 + ca) + sa
    x = x + ga * _L0_attn_ref(h, L0_attn_wq, L0_attn_wk, L0_attn_wv, L0_attn_wo)
    h = _layernorm(x, axis=-1) * (1 + cb) + sb
    x = x + gb * _L0_ffn_ref(h, L0_ffn_w_gate, L0_ffn_w_up, L0_ffn_w_down)
    return x

_drawn_inputs = setup_inputs


def setup_inputs(seed=0):
    import zlib

    import numpy as np

    out = dict(_drawn_inputs(seed))
    spreads = {}
    factors = {}
    for name, (base, spread) in spreads.items():
        noise = np.random.default_rng([zlib.crc32(name.encode()), seed]).standard_normal(out[name].shape)
        drawn = base * np.exp(spread * noise) if base else spread * noise
        out[name] = jnp.asarray(drawn.astype(out[name].dtype))
    for name, factor in factors.items():
        out[name] = (out[name] * factor).astype(out[name].dtype)
    return out
```

```python
from contextlib import ExitStack

import numpy as np
import concourse.bass as bass
from concourse import mybir

B, S, D, H, HID = 2, 1024, 512, 16, 2048
DH = D // H
P = 128
NF = D // P
NI = S // P
NT = B * NI
HC = 256
NJ = HID // HC
NM = HC // P
TC = 512
NC = B * S // TC
TPC = TC // P
EPS = 1e-5
GATE_MIN = 0.25
MASKED = -3e38

F32, F32R, BF16 = mybir.dt.float32, mybir.dt.float32r, mybir.dt.bfloat16
ALU, ACT, AX = mybir.AluOpType, mybir.ActivationFunctionType, mybir.AxisListType

KB = 1024
R1, R2, R3, R4, R5 = 0, 64 * KB, 96 * KB, 128 * KB, 192 * KB

ORDER = [7, 0, 6, 1, 5, 2, 4, 3]
STEPS = 2 * NI
PREP_AT = {2: 0, 3: 1, 4: 2, 5: 3}
PREP_ACT = (True, False, True, False)


def attention_fills(last):
    fills, group = [], 0
    for k in range(STEPS):
        if k % NI in PREP_AT and not (last and k >= NI):
            q = PREP_AT[k % NI]
            fills.append(("qk", k, q, PREP_ACT[q]))
        i = ORDER[k % NI]
        fills.append(("p", k, (0, min(4, i + 1), group), True))
        group += 1
        if i >= 4:
            fills.append(("p", k, (4, i - 3, group), False))
            group += 1
    return fills


FILLS = {last: attention_fills(last) for last in (False, True)}
last_fill = {last: [max(n for n, x in enumerate(FILLS[last]) if x[0] == "p" and x[1] == k) for k in range(STEPS)]
             for last in (False, True)}
PER_BODY = len(FILLS[False])
ACT_PER_BODY = sum(f[3] for f in FILLS[False])
DVE_PER_BODY = PER_BODY - ACT_PER_BODY
PRE = 4
NPT = 4


def emptied(h, f, last):
    if f < 0 and isinstance(h, int) and h == 0:
        q = PRE + f
        return PREP_ACT[q], sum(1 for x in PREP_ACT[:q + 1] if x == PREP_ACT[q])
    if f < 0:
        h, f, last = h - 1, f + PER_BODY, False
    fills = FILLS[last]
    on_act = fills[f][3]
    n = sum(1 for x in fills[:f + 1] if x[3] == on_act)
    per = ACT_PER_BODY if on_act else DVE_PER_BODY
    base = sum(1 for x in PREP_ACT if x == on_act)
    return on_act, h * per + base + n


def adaln_block(nc, x, c_t, wmod_a, wmod_b, wqkv, wo, wffn, cos, sin, out):
    ctx = ExitStack()
    with ctx:
        base = -(-nc.sbuf_base // 64) * 64

        def sb(name, n, dt, at):
            return nc.alloc_sbuf_tensor_at(name, [P, n], dt, offset=base + at)

        at = R5
        small = {}

        def keep(name, n, dt=F32):
            nonlocal at
            small[name] = sb(name, n, dt, at)
            at += (n * (2 if dt == BF16 else 4) + 31) // 32 * 32
            return small[name]

        ident = keep("ident", P)
        ident_r = keep("ident_r", P, F32R)
        ident_bf = keep("ident_bf", P, BF16)
        mask_bf = keep("mask_bf", P, BF16)
        cos_sb = keep("cos_sb", 2 * NI * DH)
        sin_sb = keep("sin_sb", 2 * NI * DH)
        gates = keep("gates", 2 * B * D)
        modcol = keep("modcol", 4 * NF * B)
        gatecol = keep("gatecol", 2 * NF * B)
        gatesgn = keep("gatesgn", 2 * NF * B)
        c_sb = keep("c_sb", NF * B)
        silu_c = keep("silu_c", NF * B)
        eps_sb = keep("eps_sb", 1)
        stat6 = keep("stat6", 2 * 6)
        mv = keep("mv", 2 * 2)
        std = keep("std", 2)
        rstd = keep("rstd", 2)
        negmax = keep("negmax", 4)
        rowsum = keep("rowsum", 2 * NI)
        rinv = keep("rinv", 2 * NI)
        assert base + at <= nc.sbuf_usable_end

        qk_raw = sb("qk_raw", H * 2 * NT * DH, F32, R1)
        wmod_a_sb = sb("wmod_a_sb", 4 * NF * D, F32, R1)
        wqkv_st = sb("wqkv_st", 3 * NF * D, F32, R1 + 32 * KB)
        v_raw = sb("v_raw", H * NT * DH, F32, R2)
        wmod_b_sb = sb("wmod_b_sb", 2 * NF * D, F32, R3)
        x_t = [sb(f"x_t{u}", D, F32, R3 + (16 + 2 * u) * KB) for u in range(2)]
        gate_rep = sb("gate_rep", 2 * NF * B * P, F32, R3 + 20 * KB)
        h1 = [sb(f"h1_{u}", D, F32, R3 + (28 + 2 * u) * KB) for u in range(2)]
        wqkv_hi = sb("wqkv_hi", 3 * NF * D, F32R, R4)
        wqkv_lo = sb("wqkv_lo", 3 * NF * D, F32R, R4 + 24 * KB)
        h1_hi = [sb(f"h1_hi{u}", D, F32R, R4 + (48 + 2 * u) * KB) for u in range(2)]
        h1_lo = [sb(f"h1_lo{u}", D, F32R, R4 + (52 + 2 * u) * KB) for u in range(2)]
        xn1 = [sb(f"xn1_{u}", D, F32, R4 + (56 + 2 * u) * KB) for u in range(2)]

        stack = [sb(f"stack{u}", 2 * NI * P, F32R, R4 + 8 * u * KB) for u in range(2)]
        qk_t = [sb(f"qk_t{u}", 2 * S, F32R, R4 + (16 + 8 * u) * KB) for u in range(2)]
        probs = [sb(f"probs{k}", S, F32, R4 + (32 + 4 * k) * KB) for k in range(2)]
        probs_t = [sb(f"probs_t{k}", 4 * P, F32, R4 + (40 + 2 * k) * KB) for k in range(NPT)]
        v_head = [sb(f"v_head{u}", NI * DH, F32, R4 + (48 + u) * KB) for u in range(2)]
        rope_a = sb("rope_a", 2 * NI * DH, F32, R4 + 50 * KB)
        rope_b = sb("rope_b", 2 * NI * DH, F32, R4 + 52 * KB)
        roped = sb("roped", 2 * NI * DH, F32, R4 + 54 * KB)
        wo_st = sb("wo_st", NF * D, F32, R4 + 56 * KB)
        o_all = sb("o_all", NT * D, F32, R3)

        wo_gated = sb("wo_gated", NF * D, F32, R1)
        o_tile = [sb(f"o_tile{u}", D, F32, R1 + (16 + 2 * u) * KB) for u in range(2)]
        o_hi = [sb(f"o_hi{u}", D, F32R, R1 + (20 + 2 * u) * KB) for u in range(2)]
        o_lo = [sb(f"o_lo{u}", D, F32R, R1 + (24 + 2 * u) * KB) for u in range(2)]
        xn2 = [sb(f"xn2_{u}", D, F32, R1 + (28 + 2 * u) * KB) for u in range(2)]
        h2 = [sb(f"h2_{u}", D, F32, R1 + (8 + 2 * u) * KB) for u in range(2)]
        wo_hi = [sb(f"wo_hi{b}", NF * D, F32R, R1 + (32 + 16 * b) * KB) for b in range(B)]
        wo_lo = [sb(f"wo_lo{b}", NF * D, F32R, R1 + (40 + 16 * b) * KB) for b in range(B)]
        x_res = sb("x_res", NT * D, F32, R2)
        h2_hi = sb("h2_hi", NF * B * S, F32R, R4)
        h2_lo = sb("h2_lo", NF * B * S, F32R, R4 + 32 * KB)

        GU, DN = 2 * NF * HC, NM * D
        w_gu_hi = [sb(f"w_gu_hi{v}", GU, F32R, R1 + 32 * v * KB) for v in range(2)]
        w_gu_lo = [sb(f"w_gu_lo{v}", GU, F32R, R1 + (32 * v + 8) * KB) for v in range(2)]
        w_dn_hi = [sb(f"w_dn_hi{v}", B * DN, F32R, R1 + (32 * v + 16) * KB) for v in range(2)]
        w_dn_lo = [sb(f"w_dn_lo{v}", B * DN, F32R, R1 + (32 * v + 24) * KB) for v in range(2)]
        wffn_st = sb("wffn_st", GU + DN, F32, R3)
        hidden = sb("hidden", NM * TC, F32, R3 + 12 * KB)
        hid_hi = [sb(f"hid_hi{v}", NM * TC, F32R, R3 + (16 + 8 * v) * KB) for v in range(2)]
        hid_lo = [sb(f"hid_lo{v}", NM * TC, F32R, R3 + (20 + 8 * v) * KB) for v in range(2)]
        dn_gated = sb("dn_gated", DN, F32, R5 + 1 * KB + 512)
        assert dn_gated.shape[1] * 4 <= 4 * KB

        wide = [ctx.enter_context(nc.psum_tensor(f"wide{k}", [P, 1024], F32)) for k in range(2)]
        bank = [ctx.enter_context(nc.psum_tensor(f"bank{k}", [P, 512], F32)) for k in range(4)]

        def sem(name):
            return ctx.enter_context(nc.semaphore(name))

        apart_marks = sem("apart_marks")
        consts = sem("consts")
        c_in, wmod_a_in, wmod_b_in = sem("c_in"), sem("wmod_a_in"), sem("wmod_b_in")
        wqkv_in, wo_in, rope_in = sem("wqkv_in"), sem("wo_in"), sem("rope_in")
        silu_done, mod_mm, mod_done = sem("silu_done"), sem("mod_mm"), sem("mod_done")
        gate_mm, gate_col, gate_rep_done, gate_bc, gate_done = sem("gate_mm"), sem("gate_col"), sem("gate_rep_done"), sem("gate_bc"), sem("gate_done")
        wqkv_hi_done, wqkv_lo_done = sem("wqkv_hi_done"), sem("wqkv_lo_done")
        x_in = [sem(f"x_in{u}") for u in range(2)]
        stats, aggr, std_done, rstd_done, xn_done = (sem(n) for n in ("stats", "aggr", "std_done", "rstd_done", "xn_done"))
        xn_t, h_done, hi_done, lo_done = (sem(n) for n in ("xn_t", "h_done", "hi_done", "lo_done"))
        q_mm, k_mm, v_mm = sem("q_mm"), sem("k_mm"), sem("v_mm")
        q_out, k_out, v_out = sem("q_out"), sem("k_out"), sem("v_out")
        rope_step, roped_done, stack_hi, rope_lo, stack_done, v_staged = (
            sem(n) for n in ("rope_step", "roped_done", "stack_hi", "rope_lo", "stack_done", "v_staged"))
        scores, row_max, exp_done = sem("scores"), sem("row_max"), sem("exp_done")
        filled, emptied_act, emptied_dve = sem("filled"), sem("emptied_act"), sem("emptied_dve")
        head_pv, rinv_done, head_out = sem("head_pv"), sem("rinv_done"), sem("head_out")
        wo_step, wo_ready = sem("wo_step"), sem("wo_ready")
        xr_in = sem("xr_in")
        o_staged, o_t, o_hi_done, o_lo_done = sem("o_staged"), sem("o_t"), sem("o_hi_done"), sem("o_lo_done")
        attn_mm, res_done = sem("attn_mm"), sem("res_done")
        xn2_t, h2_done, h2_hi_done, h2_lo_done = sem("xn2_t"), sem("h2_done"), sem("h2_hi_done"), sem("h2_lo_done")
        wffn_in, wffn_read, w_gu_ready, w_dn_ready = sem("wffn_in"), sem("wffn_read"), sem("w_gu_ready"), sem("w_dn_ready")
        dn_mul, dn_split, dn_ready_0 = sem("dn_mul"), sem("dn_split"), sem("dn_ready_0")
        gu_split = sem("gu_split")
        gate_ps, up_ps, silu_ps, gated = sem("gate_ps"), sem("up_ps"), sem("silu_ps"), sem("gated")
        hid_hi_done, hid_lo_done, down_ps = sem("hid_hi_done"), sem("hid_lo_done"), sem("down_ps")
        stored = sem("stored")

        block = ctx.enter_context(nc.Block())

        def after(eng, semaphore, count):
            if isinstance(count, int) and count <= 0:
                return
            eng.wait_ge(semaphore, count)

        def apart(eng):
            eng.sem_inc(apart_marks, 1)

        def after_fill(eng, h, f, last):
            on_act, count = emptied(h, f, last)
            after(eng, emptied_act if on_act else emptied_dve, count)

        x_rows = x.rearrange("(t p) d -> t p d", p=P)
        out_rows = out.rearrange("(c t p) d -> c p t d", p=P, t=TPC)

        def mod(kind, chunk, b):
            k = (kind * NF + chunk) * B + b
            return modcol[:, k:k + 1]

        SA, CA, SB, CB = range(4)

        @block.sync
        def _(sp):
            for u in range(B):
                sp.dma_start(x_t[u][:, :], x_rows[u * NI]).then_inc(x_in[u], 16)
            sp.dma_start(c_sb[:, :], c_t[:, :]).then_inc(c_in, 16)
            sp.dma_start(wmod_a_sb[:, :], wmod_a[:, :]).then_inc(wmod_a_in, 16)
            sp.dma_start(cos_sb[:, :], cos[:, :]).then_inc(rope_in, 16)
            sp.dma_start(sin_sb[:, :], sin[:, :]).then_inc(rope_in, 16)
            sp.dma_start(wmod_b_sb[:, :], wmod_b[:, :]).then_inc(wmod_b_in, 16)
            with sp.Fori(1, NI) as i:
                for u in range(B):
                    sp.wait_ge(xn_done, 2 * i + u - 1)
                    sp.dma_start(x_t[u][:, :], x[bass.ds((i + u * NI) * P, P), :]).then_inc(x_in[u], 16)
            sp.wait_ge(v_mm, NT)
            sp.dma_start(wo_st[:, :], wo[:, :]).then_inc(wo_in, 16)
            sp.wait_ge(v_staged, 2 * H)
            for b in range(B):
                sp.dma_start(x_res[:, b * NI * D:(b + 1) * NI * D].rearrange("p (t d) -> p t d", d=D),
                             x[b * S:(b + 1) * S, :].rearrange("(t p) d -> p t d", p=P)).then_inc(xr_in, 16)
            sp.wait_ge(o_staged, NT)
            sp.dma_start(wffn_st[:, :], wffn[0:P, :]).then_inc(wffn_in, 16)
            with sp.Fori(1, NJ) as j:
                sp.wait_ge(wffn_read, j)
                sp.dma_start(wffn_st[:, :], wffn[bass.ds(j * P, P), :]).then_inc(wffn_in, 16)
            for c in range(NC):
                sp.wait_ge(res_done, NT + ((NJ - 1) * NC + c + 1) * TPC)
                sp.dma_start(out_rows[c],
                             x_res[:, c * TPC * D:(c + 1) * TPC * D].rearrange("p (t d) -> p t d", d=D)
                             ).then_inc(stored, 16)
            sp.wait_ge(stored, 16 * NC)

        @block.tensor
        def _(pe):
            def mod_columns(ps, w, kinds, done):
                for kk in range(kinds):
                    for ch in range(NF):
                        for f in range(NF):
                            o = (kk * NF + ch) * B
                            w0 = (kk * NF + f) * D + ch * P
                            last = nc.tensor.matmul(ps[:, o:o + B], w[:, w0:w0 + P], silu_c[:, f * B:(f + 1) * B],
                                                    start=(f == 0), stop=(f == NF - 1))
                last.then_inc(done, 1)

            pe.wait_ge(silu_done, 1)
            pe.wait_ge(wmod_a_in, 16)
            mod_columns(bank[3], wmod_a_sb, 4, mod_mm)

            def transpose_xn(i, u):
                pe.wait_ge(xn_done, 2 * i + u + 1)
                after(pe, h_done, 2 * i + u - 1)
                for f in range(NF):
                    last = nc.tensor.transpose(bank[u][:, f * P:(f + 1) * P], xn1[u][:, f * P:(f + 1) * P], ident[:, :])
                last.then_inc(xn_t, 1)

            def project(i, u):
                pe.wait_ge(hi_done, 2 * i + u + 1)
                pe.wait_ge(lo_done, 2 * i + u + 1)
                for w, (ps, done, read) in enumerate((
                        (wide[u][:, 0:512], q_mm, q_out),
                        (wide[u][:, 512:1024], k_mm, k_out),
                        (bank[2 + u][:, :], v_mm, v_out))):
                    after(pe, read, 2 * i + u - 1)
                    n = 0
                    for a, ww in ((h1_hi, wqkv_hi), (h1_hi, wqkv_lo), (h1_lo, wqkv_hi)):
                        for f in range(NF):
                            w0 = (w * NF + f) * D
                            last = nc.tensor.matmul(ps, a[u][:, f * P:(f + 1) * P], ww[:, w0:w0 + D],
                                                    start=(n == 0), stop=(n == 3 * NF - 1))
                            n += 1
                    last.then_inc(done, 1)

            pe.wait_ge(consts, 4)
            transpose_xn(0, 0)
            pe.wait_ge(wqkv_hi_done, 3)
            pe.wait_ge(wqkv_lo_done, 3)
            pe.wait_ge(mod_done, 1)
            def project_pair(i):
                transpose_xn(i, 1)
                project(i, 0)
                transpose_xn(i + 1, 0)
                project(i, 1)

            project_pair(0)
            with pe.Fori(1, NI - 1) as i:
                project_pair(i)
            transpose_xn(NI - 1, 1)
            project(NI - 1, 0)
            project(NI - 1, 1)

            pe.wait_ge(wmod_b_in, 16)
            pe.wait_ge(v_out, NT)
            mod_columns(bank[2], wmod_b_sb, 2, gate_mm)
            pe.wait_ge(q_out, NT)
            pe.wait_ge(k_out, NT)
            pe.wait_ge(gate_rep_done, 1)
            for g in range(2 * B):
                kind, b = divmod(g, B)
                for f in range(NF):
                    r = ((kind * NF + f) * B + b) * P
                    last = nc.tensor.transpose(wide[g // 2][:, (g % 2) * 512 + f * P:(g % 2) * 512 + (f + 1) * P],
                                               gate_rep[:, r:r + P], ident[:, :])
            last.then_inc(gate_bc, 1)

            def transpose_stack(quarter, u, f):
                for t in range(4):
                    o = (quarter * 4 + t) * P
                    inst = nc.tensor.transpose(bank[f % 2][:, t * P:(t + 1) * P].bitcast(F32R), stack[u][:, o:o + P],
                                               ident_r[:, :])
                inst.then_inc(filled, 1)

            def fill_stack(f, n_ready, u, quarter, h, last):
                pe.wait_ge(stack_done, n_ready)
                after_fill(pe, h, f - 2, last)
                transpose_stack(quarter, u, f)

            def score(h, k, last):
                u, i = k // NI, ORDER[k % NI]
                after(pe, exp_done, h * STEPS + k - 1)
                if k % NI == 0:
                    for q in (2, 3):
                        if k == 0:
                            after_fill(pe, h, -PRE + q if isinstance(h, int) and h == 0 else
                                       [n for n, x in enumerate(FILLS[False]) if x[0] == "qk"][4 + q] - PER_BODY, False)
                        else:
                            after_fill(pe, h, [n for n, x in enumerate(FILLS[last]) if x[0] == "qk"][q], last)
                ps = wide[k % 2]
                n = (i + 1) * P
                for a in range(0, n, 512):
                    e = min(n, a + 512)
                    diag = e == n
                    inst = nc.tensor.matmul(ps[:, a:e], qk_t[u][:, i * P:(i + 1) * P], qk_t[u][:, S + a:S + e],
                                            start=True, stop=not diag)
                inst = nc.tensor.matmul(ps[:, n - P:n], ident_bf[:, :], mask_bf[:, :], start=False, stop=True)
                inst.then_inc(scores, 1)

            def fill_probs(h, f, k, first_block, blocks, last):
                after_fill(pe, h, f - 2, last)
                if first_block == 0:
                    pe.wait_ge(exp_done, h * STEPS + k + 1)
                for j in range(blocks):
                    c0 = (first_block + j) * P
                    inst = nc.tensor.transpose(bank[f % 2][:, j * P:(j + 1) * P], probs[k % 2][:, c0:c0 + P], ident[:, :])
                inst.then_inc(filled, 1)

            def weigh_values(h, f, k, first_block, blocks, group, last):
                u, i = k // NI, ORDER[k % NI]
                after_fill(pe, h, f, last)
                if k % NI == 0 and first_block == 0:
                    pe.wait_ge(v_staged, 2 * h + u + 1)
                    after(pe, head_out, 2 * h + u - 1)
                for j in range(blocks):
                    kt = first_block + j
                    inst = nc.tensor.matmul(bank[2 + u][:, i * DH:(i + 1) * DH], probs_t[group % NPT][:, j * P:(j + 1) * P],
                                            v_head[u][:, kt * DH:(kt + 1) * DH], start=(kt == 0), stop=(kt == i))
                if k % NI == NI - 1 and first_block + blocks == i + 1:
                    inst.then_inc(head_pv, 1)

            def attend(h, first, last):
                fills = FILLS[last]
                pending = None
                if not first:
                    kind, k, arg, _ = FILLS[False][-1]
                    pending = (h - 1, PER_BODY - 1, k, *arg, False)
                f = 0
                for k in range(STEPS):
                    if k < STEPS - 2:
                        score(h, k + 2, last)
                    elif not last:
                        score(h + 1, k + 2 - STEPS, False)
                    while f < len(fills) and fills[f][1] == k:
                        kind, _, arg, _ = fills[f]
                        if kind == "qk":
                            u = 1 - k // NI
                            fill_stack(f, 2 * h + k // NI + 2, u, arg, h, last)
                        else:
                            fill_probs(h, f, k, arg[0], arg[1], last)
                            if pending:
                                weigh_values(*pending)
                            pending = (h, f, k, *arg, last)
                        f += 1
                return pending

            pe.wait_ge(gate_done, 1)
            for q in range(PRE):
                after(pe, stack_done, 1)
                if q >= 2:
                    after_fill(pe, 0, q - 2 - PRE, False)
                transpose_stack(q, 0, q)
            score(0, 0, False)
            score(0, 1, False)
            attend(0, True, False)
            with pe.Fori(1, H - 1) as h:
                attend(h, False, False)
            weigh_values(*attend(H - 1, False, True))

            def transpose_o(i, u):
                pe.wait_ge(o_staged, 2 * i + u + 1)
                after(pe, o_lo_done, 2 * i + u - 1)
                for f in range(NF):
                    inst = nc.tensor.transpose(bank[u][:, f * P:(f + 1) * P], o_tile[u][:, f * P:(f + 1) * P], ident[:, :])
                inst.then_inc(o_t, 1)

            def project_out(i, u):
                pe.wait_ge(o_hi_done, 2 * i + u + 1)
                pe.wait_ge(o_lo_done, 2 * i + u + 1)
                after(pe, res_done, 2 * i + u - 1)
                n = 0
                for a, w in ((o_hi, wo_hi), (o_hi, wo_lo), (o_lo, wo_hi)):
                    for f in range(NF):
                        inst = nc.tensor.matmul(bank[2 + u][:, :], a[u][:, f * P:(f + 1) * P], w[u][:, f * D:(f + 1) * D],
                                                start=(n == 0), stop=(n == 3 * NF - 1))
                        n += 1
                inst.then_inc(attn_mm, 1)

            def transpose_xn2(i, u):
                pe.wait_ge(xn_done, NT + 2 * i + u + 1)
                after(pe, h2_done, 2 * i + u - 1)
                for f in range(NF):
                    inst = nc.tensor.transpose(wide[u][:, f * P:(f + 1) * P], xn2[u][:, f * P:(f + 1) * P], ident[:, :])
                inst.then_inc(xn2_t, 1)

            pe.wait_ge(head_out, 2 * H)
            transpose_o(0, 0)
            pe.wait_ge(wo_ready, 2)
            transpose_o(0, 1)
            project_out(0, 0)
            def project_out_pair(i):
                transpose_o(i + 1, 0)
                project_out(i, 1)
                transpose_xn2(i, 0)
                transpose_o(i + 1, 1)
                project_out(i + 1, 0)
                transpose_xn2(i, 1)

            project_out_pair(0)
            with pe.Fori(1, NI - 1) as i:
                project_out_pair(i)
            project_out(NI - 1, 1)
            transpose_xn2(NI - 1, 0)
            transpose_xn2(NI - 1, 1)

            def gate_up(w, v, c):
                for m in range(NM):
                    for side, (ps, done, read) in enumerate(((wide[0], gate_ps, silu_ps), (wide[1], up_ps, gated))):
                        after(pe, read, NM * (w - 1) + m + 1)
                        n = 0
                        for ww, a in ((w_gu_hi, h2_hi), (w_gu_lo, h2_hi), (w_gu_hi, h2_lo)):
                            for f in range(NF):
                                w0 = (side * NF + f) * HC + m * P
                                a0 = f * B * S + c * TC
                                inst = nc.tensor.matmul(ps[:, m * TC:(m + 1) * TC], ww[v][:, w0:w0 + P], a[:, a0:a0 + TC],
                                                        start=(n == 0), stop=(n == 3 * NF - 1))
                                n += 1
                        inst.then_inc(done, 1)

            def down(w, v, c):
                b, p = c // (NC // B), c % 2
                pe.wait_ge(hid_hi_done, w + 1)
                pe.wait_ge(hid_lo_done, w + 1)
                for t in range(TPC):
                    pe.wait_ge(res_done, NT + TPC * (w - 1) + t + 1)
                    n = 0
                    for a, ww in ((hid_hi, w_dn_hi), (hid_hi, w_dn_lo), (hid_lo, w_dn_hi)):
                        for m in range(NM):
                            inst = nc.tensor.matmul(bank[t][:, :], a[p][:, m * TC + t * P:m * TC + (t + 1) * P],
                                                    ww[v][:, (b * NM + m) * D:(b * NM + m + 1) * D],
                                                    start=(n == 0), stop=(n == 3 * NM - 1))
                            n += 1
                    inst.then_inc(down_ps, 1)

            pe.wait_ge(h2_hi_done, NT)
            pe.wait_ge(h2_lo_done, NT)
            pe.wait_ge(res_done, NT)
            def slice_pair(jj, last):
                for n in range(2 * NC):
                    w, v, c = jj * 2 * NC + n, n // NC, n % NC
                    if not (last and n == 2 * NC - 1):
                        v1, c1 = (n + 1) // NC % 2, (n + 1) % NC
                        if c1 == 0:
                            pe.wait_ge(w_gu_ready, jj * 2 + v + 2)
                        gate_up(w + 1, v1, c1)
                    if c == 0:
                        pe.wait_ge(w_dn_ready, jj * 2 + v + 1)
                    down(w, v, c)

            pe.wait_ge(w_gu_ready, 1)
            gate_up(0, 0, 0)
            with pe.Fori(0, NJ // 2 - 1) as jj:
                slice_pair(jj, False)
            slice_pair(NJ // 2 - 1, True)

        @block.scalar
        def _(act):
            act.dma_start(wqkv_st[:, :], wqkv[:, :]).then_inc(wqkv_in, 16)
            act.wait_ge(c_in, 16)
            nc.scalar.activation(silu_c[:, :], c_sb[:, :], ACT.Silu).then_inc(silu_done, 1)

            def std_of(u, count):
                act.wait_ge(aggr, count)
                nc.scalar.activation(std[:, u:u + 1], mv[:, 2 * u + 1:2 * u + 2], ACT.Sqrt,
                                     bias=eps_sb[:, 0:1]).then_inc(std_done, 1)

            def modulate(i, u):
                act.wait_ge(xn_t, 2 * i + u + 1)
                after(act, lo_done, 2 * i + u - 1)
                after(act, v_mm, 2 * i + u - 1)
                for f in range(NF):
                    inst = nc.scalar.activation(h1[u][:, f * P:(f + 1) * P], bank[u][:, f * P:(f + 1) * P], ACT.Identity,
                                                bias=mod(SA, f, u), scale=mod(CA, f, u))
                inst.then_inc(h_done, 1)
                act.wait_ge(h_done, 2 * i + u + 1)
                nc.scalar.activation(h1_hi[u][:, :], h1[u][:, :], ACT.Copy).then_inc(hi_done, 1)

            def store_qk(i, u):
                o = (i + u * NI) * DH
                view = qk_raw[:, :].rearrange("p (h w n) -> p h w n", h=H, w=2)
                for which, (mm, done) in enumerate(((q_mm, q_out), (k_mm, k_out))):
                    act.wait_ge(mm, 2 * i + u + 1)
                    nc.scalar.activation(view[:, :, which, bass.ds(o, DH)],
                                         wide[u][:, which * 512:(which + 1) * 512].rearrange("p (h d) -> p h d", d=DH),
                                         ACT.Copy).then_inc(done, 1)

            act.wait_ge(consts, 4)
            std_of(0, 1)
            std_of(1, 2)
            act.wait_ge(wqkv_in, 16)
            for w in range(3):
                nc.scalar.activation(wqkv_hi[:, w * NF * D:(w + 1) * NF * D], wqkv_st[:, w * NF * D:(w + 1) * NF * D],
                                     ACT.Copy).then_inc(wqkv_hi_done, 1)
            act.wait_ge(mod_done, 1)
            modulate(0, 0)

            def pair1(i):
                std_of(0, 2 * i + 3)
                modulate(i, 1)
                store_qk(i, 0)
                std_of(1, 2 * i + 4)
                modulate(i + 1, 0)
                store_qk(i, 1)

            pair1(0)
            with act.Fori(1, NI - 1) as i:
                pair1(i)
            modulate(NI - 1, 1)
            store_qk(NI - 1, 0)
            store_qk(NI - 1, 1)

            def empty(h, f, last):
                kind, k, arg, _ = FILLS[last][f]
                act.wait_ge(filled, h * PER_BODY + PRE + f + 1)
                if kind == "qk":
                    dst = qk_t[1 - k // NI][:, arg * 512:(arg + 1) * 512]
                    nc.scalar.activation(dst, bank[f % 2][:, :], ACT.Copy).then_inc(emptied_act, 1)
                else:
                    n = arg[1] * P
                    nc.scalar.activation(probs_t[arg[2] % NPT][:, 0:n], bank[f % 2][:, 0:n], ACT.Copy).then_inc(emptied_act, 1)

            def exponentials(h, k, last):
                if k >= 2:
                    after(act, filled, h * PER_BODY + PRE + last_fill[last][k - 2] + 1)
                elif not isinstance(h, int) or h:
                    after(act, filled, (h - 1) * PER_BODY + PRE + last_fill[False][k - 2] + 1)
                u, i = k // NI, ORDER[k % NI]
                n = (i + 1) * P
                act.wait_ge(row_max, h * STEPS + k + 1)
                if k % NI == 0:
                    after(act, head_out, 2 * h + u - 1)
                nc.scalar.activation(probs[k % 2][:, 0:n], wide[k % 2][:, 0:n], ACT.Exp, bias=negmax[:, k % 4:k % 4 + 1],
                                     accum_out=rowsum[:, u * NI + i:u * NI + i + 1]).then_inc(exp_done, 1)

            def attend(h, last):
                for k in range(STEPS):
                    if k < STEPS - 1:
                        exponentials(h, k + 1, last)
                    elif not last:
                        exponentials(h + 1, 0, False)
                    for f, x_ in enumerate(FILLS[last]):
                        if x_[1] == k and x_[3]:
                            empty(h, f, last)

            act.wait_ge(v_out, NT)
            for q in (0, 2):
                act.wait_ge(filled, q + 1)
                nc.scalar.activation(qk_t[0][:, q * 512:(q + 1) * 512], bank[q % 2][:, :], ACT.Copy).then_inc(emptied_act, 1)
            exponentials(0, 0, False)
            attend(0, False)
            with act.Fori(1, H - 1) as h:
                attend(h, False)
            attend(H - 1, True)

            def high_o(i, u):
                act.wait_ge(o_t, 2 * i + u + 1)
                after(act, attn_mm, 2 * i + u - 1)
                nc.scalar.activation(o_hi[u][:, :], bank[u][:, :], ACT.Copy).then_inc(o_hi_done, 1)

            def modulate2(i, u):
                act.wait_ge(xn2_t, 2 * i + u + 1)
                after(act, h2_lo_done, 2 * i + u - 1)
                for f in range(NF):
                    inst = nc.scalar.activation(h2[u][:, f * P:(f + 1) * P], wide[u][:, f * P:(f + 1) * P], ACT.Identity,
                                                bias=mod(SB, f, u), scale=mod(CB, f, u))
                inst.then_inc(h2_done, 1)
                act.wait_ge(h2_done, 2 * i + u + 1)
                nc.scalar.activation(h2_hi[:, :].rearrange("p (f n) -> p f n", f=NF)[:, :, bass.ds((i + u * NI) * P, P)],
                                     h2[u][:, :].rearrange("p (f n) -> p f n", f=NF), ACT.Copy).then_inc(h2_hi_done, 1)

            act.wait_ge(head_out, 2 * H)
            act.wait_ge(wo_ready, 2)
            high_o(0, 0)
            high_o(0, 1)
            def pair3(i):
                std_of(0, NT + 2 * i + 1)
                high_o(i + 1, 0)
                modulate2(i, 0)
                std_of(1, NT + 2 * i + 2)
                high_o(i + 1, 1)
                modulate2(i, 1)

            pair3(0)
            with act.Fori(1, NI - 1) as i:
                pair3(i)
            for u in range(2):
                std_of(u, NT + 2 * (NI - 1) + u + 1)
            for u in range(2):
                modulate2(NI - 1, u)

            def unit(w, p):
                for m in range(NM):
                    act.wait_ge(gate_ps, NM * w + m + 1)
                    after(act, hid_lo_done, w)
                    nc.scalar.activation(hidden[:, m * TC:(m + 1) * TC], wide[0][:, m * TC:(m + 1) * TC],
                                         ACT.Silu).then_inc(silu_ps, 1)
                act.wait_ge(gated, NM * (w + 1))
                after(act, down_ps, TPC * (w - 1))
                nc.scalar.activation(hid_hi[p][:, :], hidden[:, :], ACT.Copy).then_inc(hid_hi_done, 1)

            act.wait_ge(o_staged, NT)
            unit(0, 0)
            unit(1, 1)
            with act.Fori(1, NJ * NC // 2) as ww:
                unit(2 * ww, 0)
                unit(2 * ww + 1, 1)

        @block.vector
        def _(dve):
            def normalise(src, dst, u, count):
                apart(dve)
                nc.vector.bn_stats(stat6[:, 6 * u:6 * u + 6], src).then_inc(stats, 1)
                dve.wait_ge(stats, count)
                apart(dve)
                nc.vector.bn_aggr(mv[:, 2 * u:2 * u + 2], stat6[:, 6 * u:6 * u + 6]).then_inc(aggr, 1)
                dve.wait_ge(std_done, count)
                nc.vector.reciprocal(rstd[:, u:u + 1], std[:, u:u + 1]).then_inc(rstd_done, 1)
                dve.wait_ge(rstd_done, count)
                nc.vector.tensor_scalar(dst, src, mv[:, 2 * u:2 * u + 1], rstd[:, u:u + 1], ALU.subtract, ALU.mult
                                        ).then_inc(xn_done, 1)

            def norm1(i, u):
                dve.wait_ge(x_in[u], 16 * (i + 1))
                after(dve, xn_t, 2 * i + u - 1)
                normalise(x_t[u][:, :], xn1[u][:, :], u, 2 * i + u + 1)

            def store_v(i, u):
                dve.wait_ge(v_mm, 2 * i + u + 1)
                nc.vector.tensor_copy(v_raw[:, :].rearrange("p (h n) -> p h n", h=H)[:, :, bass.ds((i + u * NI) * DH, DH)],
                                      bank[2 + u][:, :].rearrange("p (h d) -> p h d", d=DH)).then_inc(v_out, 1)

            dve.wait_ge(consts, 4)
            norm1(0, 0)
            norm1(0, 1)
            dve.wait_ge(mod_mm, 1)
            one_plus = modcol[:, :].rearrange("p (k n) -> p k n", k=4)
            ps_kinds = bank[3][:, 0:4 * NF * B].rearrange("p (k n) -> p k n", k=4)
            for kind in range(4):
                inst = nc.vector.tensor_scalar(one_plus[:, kind], ps_kinds[:, kind], float(kind in (CA, CB)), None, ALU.add)
            inst.then_inc(mod_done, 1)
            for w in range(3):
                dve.wait_ge(wqkv_hi_done, w + 1)
                seg = slice(w * NF * D, (w + 1) * NF * D)
                nc.vector.tensor_tensor(wqkv_lo[:, seg], wqkv_st[:, seg], wqkv_hi[:, seg].bitcast(F32), ALU.subtract
                                        ).then_inc(wqkv_lo_done, 1)
            with dve.Fori(0, NI - 1) as i:
                norm1(i + 1, 0)
                store_v(i, 0)
                norm1(i + 1, 1)
                store_v(i, 1)
            store_v(NI - 1, 0)
            store_v(NI - 1, 1)

            dve.wait_ge(gate_mm, 1)
            gps = bank[2][:, 0:2 * NF * B]
            nc.vector.tensor_scalar(gatesgn[:, :], gps, 0.0, 2.0, ALU.is_ge, ALU.mult).then_inc(gate_col, 1)
            dve.wait_ge(gate_col, 1)
            nc.vector.tensor_scalar(gatesgn[:, :], gatesgn[:, :], -1.0, None, ALU.add).then_inc(gate_col, 1)
            dve.wait_ge(gate_col, 2)
            nc.vector.tensor_tensor(gatecol[:, :], gps, gatesgn[:, :], ALU.mult).then_inc(gate_col, 1)
            dve.wait_ge(gate_col, 3)
            nc.vector.tensor_scalar(gatecol[:, :], gatecol[:, :], GATE_MIN, None, ALU.max).then_inc(gate_col, 1)
            dve.wait_ge(gate_col, 4)
            nc.vector.tensor_tensor(gatecol[:, :], gatecol[:, :], gatesgn[:, :], ALU.mult).then_inc(gate_col, 1)
            dve.wait_ge(gate_col, 5)
            nc.vector.tensor_copy(gate_rep[:, :].rearrange("p (g r) -> p g r", r=P),
                                  gatecol[:, :].unsqueeze(2).broadcast_to([P, 2 * NF * B, P])).then_inc(gate_rep_done, 1)
            dve.wait_ge(gate_bc, 1)
            for g in range(2):
                inst = nc.vector.tensor_copy(gates[:, g * 1024:(g + 1) * 1024], wide[g][:, :])
            inst.then_inc(gate_done, 1)

            def empty(h, f, last):
                kind, k, arg, _ = FILLS[last][f]
                dve.wait_ge(filled, h * PER_BODY + PRE + f + 1)
                if kind == "qk":
                    dst = qk_t[1 - k // NI][:, arg * 512:(arg + 1) * 512]
                    nc.vector.tensor_copy(dst, bank[f % 2][:, :]).then_inc(emptied_dve, 1)
                else:
                    n = arg[1] * P
                    nc.vector.tensor_copy(probs_t[arg[2] % NPT][:, 0:n], bank[f % 2][:, 0:n]).then_inc(emptied_dve, 1)

            def maxima(h, k):
                n = (ORDER[k % NI] + 1) * P
                dve.wait_ge(scores, h * STEPS + k + 1)
                nc.vector.tensor_reduce(negmax[:, k % 4:k % 4 + 1], wide[k % 2][:, 0:n], AX.X, ALU.max, negate=True
                                        ).then_inc(row_max, 1)

            def head_output(h, u):
                dve.wait_ge(head_pv, 2 * h + u + 1)
                nc.vector.reciprocal(rinv[:, u * NI:(u + 1) * NI], rowsum[:, u * NI:(u + 1) * NI]).then_inc(rinv_done, 1)
                dve.wait_ge(rinv_done, 2 * h + u + 1)
                dst = o_all[:, u * NI * D:(u + 1) * NI * D].rearrange("p (i n) -> p i n", i=NI)[:, :, bass.ds(h * DH, DH)]
                nc.vector.tensor_tensor(dst, bank[2 + u][:, 0:NI * DH].rearrange("p (i d) -> p i d", d=DH),
                                        rinv[:, u * NI:(u + 1) * NI].unsqueeze(2).broadcast_to([P, NI, DH]), ALU.mult
                                        ).then_inc(head_out, 1)

            def attend(h, first, last):
                for k in range(STEPS):
                    if k < STEPS - 2:
                        maxima(h, k + 2)
                    elif not last:
                        maxima(h + 1, k + 2 - STEPS)
                    for f, x_ in enumerate(FILLS[last]):
                        if x_[1] == k and not x_[3]:
                            empty(h, f, last)
                    if k == 1 and not first:
                        head_output(h - 1, 1)
                    if k == NI + 1:
                        head_output(h, 0)
                    n, u = (2 * h + 1, 1) if k < NI else (2 * h + 2, 0)
                    if not (last and u == 0):
                        if k % NI == 0:
                            stack_high(n, u)
                        if k % NI == 1:
                            stack_low(n, u)

            def stack_parts(u, src, q_parts, k_parts, done):
                st = stack[u][:, :].rearrange("p (w t s d) -> p w t s d", w=2, s=4, d=DH)
                src = src.rearrange("p (w t d) -> p w t d", w=2, d=DH)
                for w, parts in enumerate((q_parts, k_parts)):
                    inst = nc.vector.tensor_copy(st[:, w, :, parts], src[:, w].unsqueeze(2).broadcast_to([P, NI, 2, DH]))
                inst.then_inc(done, 1)

            def stack_high(n, u):
                dve.wait_ge(roped_done, n + 1)
                stack_parts(u, roped[:, :], slice(0, 2), slice(0, 3, 2), stack_hi)

            def stack_low(n, u):
                dve.wait_ge(rope_lo, n + 1)
                stack_parts(u, rope_a[:, :], slice(2, 4), slice(1, 4, 2), stack_done)

            dve.wait_ge(v_mm, NT)
            stack_high(0, 0)
            stack_low(0, 0)
            for q in (1, 3):
                dve.wait_ge(filled, q + 1)
                nc.vector.tensor_copy(qk_t[0][:, q * 512:(q + 1) * 512], bank[q % 2][:, :]).then_inc(emptied_dve, 1)
            maxima(0, 0)
            maxima(0, 1)
            attend(0, True, False)
            with dve.Fori(1, H - 1) as h:
                attend(h, False, False)
            attend(H - 1, False, True)
            head_output(H - 1, 1)

            def low_o(i, u):
                dve.wait_ge(o_hi_done, 2 * i + u + 1)
                after(dve, attn_mm, 2 * i + u - 1)
                nc.vector.tensor_tensor(o_lo[u][:, :], bank[u][:, :], o_hi[u][:, :].bitcast(F32), ALU.subtract
                                        ).then_inc(o_lo_done, 1)

            def residual(i, u):
                tile = x_res[:, bass.ds((i + u * NI) * D, D)]
                dve.wait_ge(attn_mm, 2 * i + u + 1)
                nc.vector.tensor_tensor(tile, bank[2 + u][:, :], tile, ALU.add).then_inc(res_done, 1)
                dve.wait_ge(res_done, 2 * i + u + 1)
                after(dve, xn2_t, 2 * i + u - 1)
                normalise(tile, xn2[u][:, :], u, NT + 2 * i + u + 1)

            dve.wait_ge(xr_in, 16 * B)
            low_o(0, 0)
            low_o(0, 1)
            def pair3(i):
                residual(i, 0)
                low_o(i + 1, 0)
                residual(i, 1)
                low_o(i + 1, 1)

            pair3(0)
            with dve.Fori(1, NI - 1) as i:
                pair3(i)
            for u in range(2):
                residual(NI - 1, u)

            def gate_hidden(w):
                for m in range(NM):
                    seg = slice(m * TC, (m + 1) * TC)
                    dve.wait_ge(up_ps, NM * w + m + 1)
                    dve.wait_ge(silu_ps, NM * w + m + 1)
                    nc.vector.tensor_tensor(hidden[:, seg], wide[1][:, seg], hidden[:, seg], ALU.mult).then_inc(gated, 1)

            def accumulate(w, c):
                for t in range(TPC):
                    tile = x_res[:, (c * TPC + t) * D:(c * TPC + t + 1) * D]
                    dve.wait_ge(down_ps, TPC * w + t + 1)
                    nc.vector.tensor_tensor(tile, bank[t][:, :], tile, ALU.add).then_inc(res_done, 1)

            def slice_pair(jj, last):
                for n in range(2 * NC):
                    w = jj * 2 * NC + n
                    if not (last and n == 2 * NC - 1):
                        gate_hidden(w + 1)
                    accumulate(w, n % NC)

            gate_hidden(0)
            with dve.Fori(0, NJ // 2 - 1) as jj:
                slice_pair(jj, False)
            slice_pair(NJ // 2 - 1, True)

        @block.gpsimd
        def _(pool):
            pool.memset(ident[:, :], 0.0).then_inc(consts, 1)
            pool.wait_ge(consts, 1)
            pool.affine_select(out=ident[:, :], in_=ident[:, :], compare_op=ALU.not_equal, fill=1.0,
                               base=0, pattern=[[-1, P]], channel_multiplier=1).then_inc(consts, 1)
            pool.memset(eps_sb[:, :], EPS)
            pool.memset(mask_bf[:, :], 0.0).then_inc(consts, 1)
            pool.wait_ge(consts, 3)
            pool.tensor_copy(ident_bf[:, :], ident[:, :])
            pool.tensor_copy(ident_r[:, :], ident[:, :])
            pool.affine_select(out=mask_bf[:, :], in_=mask_bf[:, :], compare_op=ALU.is_ge, fill=MASKED,
                               base=0, pattern=[[-1, P]], channel_multiplier=1).then_inc(consts, 1)

            def low_h(i, u):
                pool.wait_ge(hi_done, 2 * i + u + 1)
                after(pool, v_mm, 2 * i + u - 1)
                nc.gpsimd.tensor_tensor(h1_lo[u][:, :], h1[u][:, :], h1_hi[u][:, :].bitcast(F32), ALU.subtract
                                        ).then_inc(lo_done, 1)

            for u in range(2):
                low_h(0, u)
            with pool.Fori(1, NI) as i:
                for u in range(2):
                    low_h(i, u)

            def stage_head(h, u):
                n = 2 * h + u
                raw = qk_raw[:, bass.ds(h * 2 * NT * DH, 2 * NT * DH)].rearrange(
                    "p (w n) -> p w n", w=2)[:, :, u * NI * DH:(u + 1) * NI * DH]
                raw_pair = raw.rearrange("p w (n two) -> p w n two", two=2)
                tab, pair = "p (w n) -> p w n", "p (w n two) -> p w n two"
                after(pool, stack_done, n)
                pool.tensor_tensor(rope_a[:, :].rearrange(tab, w=2), raw, cos_sb[:, :].rearrange(tab, w=2), ALU.mult)
                for odd in range(2):
                    inst = pool.tensor_tensor(rope_b[:, :].rearrange(pair, w=2, two=2)[:, :, :, odd],
                                              raw_pair[:, :, :, 1 - odd],
                                              sin_sb[:, :].rearrange(pair, w=2, two=2)[:, :, :, odd], ALU.mult)
                inst.then_inc(rope_step, 1)
                pool.wait_ge(rope_step, n + 1)
                pool.tensor_tensor(roped[:, :], rope_a[:, :], rope_b[:, :], ALU.add).then_inc(roped_done, 1)
                after(pool, head_pv, n - 1)
                apart(pool)
                pool.tensor_copy(v_head[u][:, :], v_raw[:, bass.ds(h * NT * DH + u * NI * DH, NI * DH)]
                                 ).then_inc(v_staged, 1)
                pool.wait_ge(stack_hi, n + 1)
                for w in range(2):
                    seg = slice(w * NI * DH, (w + 1) * NI * DH)
                    hi = stack[u][:, :].rearrange("p (w t s d) -> p w t s d", w=2, s=4, d=DH)[:, w, :, 0]
                    inst = pool.tensor_tensor(rope_a[:, seg].rearrange("p (t d) -> p t d", d=DH),
                                              roped[:, seg].rearrange("p (t d) -> p t d", d=DH), hi.bitcast(F32),
                                              ALU.subtract)
                inst.then_inc(rope_lo, 1)

            pool.wait_ge(rope_in, 32)
            pool.wait_ge(q_out, NT)
            pool.wait_ge(k_out, NT)
            pool.wait_ge(v_out, NT)
            for u in range(B):
                stage_head(0, u)
            with pool.Fori(1, H) as h:
                for u in range(B):
                    stage_head(h, u)

            pool.wait_ge(wo_in, 16)
            pool.wait_ge(gate_done, 1)
            for b in range(B):
                g = gates[:, b * D:(b + 1) * D]
                after(pool, wo_ready, b)
                for f in range(NF):
                    seg = slice(f * D, (f + 1) * D)
                    inst = pool.tensor_tensor(wo_gated[:, seg], wo_st[:, seg], g, ALU.mult)
                inst.then_inc(wo_step, 1)
                pool.wait_ge(wo_step, 2 * b + 1)
                pool.tensor_copy(wo_hi[b][:, :], wo_gated[:, :]).then_inc(wo_step, 1)
                pool.wait_ge(wo_step, 2 * b + 2)
                pool.tensor_tensor(wo_lo[b][:, :], wo_gated[:, :], wo_hi[b][:, :].bitcast(F32), ALU.subtract
                                   ).then_inc(wo_ready, 1)

            def stage_o(i, u):
                after(pool, o_t, 2 * i + u - 1)
                apart(pool)
                pool.tensor_copy(o_tile[u][:, :], o_all[:, bass.ds((i + u * NI) * D, D)]).then_inc(o_staged, 1)

            def low_h2(i, u):
                pool.wait_ge(h2_hi_done, 2 * i + u + 1)
                seg = bass.ds((i + u * NI) * P, P)
                hi = h2_hi[:, :].rearrange("p (f n) -> p f n", f=NF)[:, :, seg]
                lo = h2_lo[:, :].rearrange("p (f n) -> p f n", f=NF)[:, :, seg]
                pool.tensor_tensor(lo, h2[u][:, :].rearrange("p (f n) -> p f n", f=NF), hi.bitcast(F32), ALU.subtract
                                   ).then_inc(h2_lo_done, 1)

            pool.wait_ge(head_out, 2 * H)
            stage_o(0, 0)
            stage_o(0, 1)
            with pool.Fori(0, NI - 1) as i:
                for u in range(2):
                    stage_o(i + 1, u)
                for u in range(2):
                    low_h2(i, u)
            for u in range(2):
                low_h2(NI - 1, u)

            def stage_slice(j, v, part):
                gu = wffn_st[:, 0:GU]
                if part == 0:
                    pool.wait_ge(wffn_in, 16 * (j + 1))
                    after(pool, down_ps, (j - 1) * NC * TPC)
                    apart(pool)
                    pool.tensor_copy(w_gu_hi[v][:, :], gu).then_inc(gu_split, 1)
                elif part == 1:
                    pool.wait_ge(gu_split, j + 1)
                    pool.tensor_tensor(w_gu_lo[v][:, :], gu, w_gu_hi[v][:, :].bitcast(F32), ALU.subtract
                                       ).then_inc(w_gu_ready, 1)
                else:
                    b = part - 2
                    g = gates[:, (B + b) * D:(B + b + 1) * D]
                    seg = slice(b * DN, (b + 1) * DN)
                    if b == 1:
                        pool.wait_ge(dn_ready_0, j + 1)
                    multiplied, split = ((dn_mul, dn_ready_0), (wffn_read, w_dn_ready))[b]
                    for m in range(NM):
                        inst = pool.tensor_tensor(dn_gated[:, m * D:(m + 1) * D],
                                                  wffn_st[:, GU + m * D:GU + (m + 1) * D], g, ALU.mult)
                    inst.then_inc(multiplied, 1)
                    pool.wait_ge(multiplied, j + 1)
                    apart(pool)
                    pool.tensor_copy(w_dn_hi[v][:, seg], dn_gated[:, :]).then_inc(dn_split, 1)
                    pool.wait_ge(dn_split, 2 * j + b + 1)
                    pool.tensor_tensor(w_dn_lo[v][:, seg], dn_gated[:, :], w_dn_hi[v][:, seg].bitcast(F32), ALU.subtract
                                       ).then_inc(split, 1)

            def low_hidden(w, p):
                pool.wait_ge(hid_hi_done, w + 1)
                after(pool, down_ps, TPC * (w - 1))
                pool.tensor_tensor(hid_lo[p][:, :], hidden[:, :], hid_hi[p][:, :].bitcast(F32), ALU.subtract
                                   ).then_inc(hid_lo_done, 1)

            def slice_units(j, stage_v):
                for c in range(NC):
                    low_hidden(j * NC + c, c % 2)
                    if stage_v is not None:
                        stage_slice(j + 1, stage_v, c)

            pool.wait_ge(h2_hi_done, NT)
            for part in range(4):
                stage_slice(0, 0, part)
            slice_units(0, 1)
            with pool.Fori(0, NJ // 2 - 1) as jj:
                slice_units(2 * jj + 1, 0)
                slice_units(2 * jj + 2, 1)
            slice_units(NJ - 1, None)


def kernel(L0_attn_x, L0_attn_wq, L0_attn_wk, L0_attn_wv, L0_attn_wo, L0_ffn_w_gate, L0_ffn_w_up, L0_ffn_w_down,
           L0_c, L0_wmod):
    import concourse.bacc as _bacc
    from concourse.bass_utils import run_bass_kernel_spmd as _run

    def rows(w):
        w = np.asarray(w)
        return w.reshape(w.shape[0] // P, P, w.shape[1]).transpose(1, 0, 2)

    wq, wk, wv, wo = (rows(np.asarray(w).T) for w in (L0_attn_wq, L0_attn_wk, L0_attn_wv, L0_attn_wo))
    wmod = np.asarray(L0_wmod).reshape(NF, P, 6, D).transpose(1, 2, 0, 3)
    sides = [np.asarray(w).T.reshape(NF, P, NJ, HC).transpose(2, 1, 0, 3).reshape(NJ, P, NF * HC)
             for w in (L0_ffn_w_gate, L0_ffn_w_up)]
    down = np.asarray(L0_ffn_w_down).T.reshape(NJ, NM, P, D).transpose(0, 2, 1, 3).reshape(NJ, P, NM * D)

    inv_freq = np.float32(10000.0) ** (np.float32(-2.0) * np.arange(DH // 2, dtype=np.float32) / np.float32(DH))
    ang = (np.arange(S, dtype=np.float32)[:, None] * inv_freq[None, :]).astype(np.float32)
    scale = np.array([1.0 / np.sqrt(np.float32(DH)), 1.0], np.float32)
    sign = np.tile(np.array([-1.0, 1.0], np.float32), DH // 2)

    def table(t, s):
        t = (np.repeat(t, 2, axis=-1) * s).astype(np.float32)
        t = scale[:, None, None] * t[None]
        return t.reshape(2, NI, P, DH).transpose(2, 0, 1, 3).reshape(P, 2 * NI * DH)

    arrays = {
        "x": np.asarray(L0_attn_x).reshape(B * S, D),
        "c_t": np.asarray(L0_c).T.reshape(NF, P, B).transpose(1, 0, 2).reshape(P, NF * B),
        "wmod_a": wmod[:, [0, 1, 3, 4]].reshape(P, -1),
        "wmod_b": wmod[:, [2, 5]].reshape(P, -1),
        "wqkv": np.stack([wq, wk, wv], 1).reshape(P, -1),
        "wo": wo.reshape(P, -1),
        "wffn": np.concatenate([*sides, down], axis=2).reshape(NJ * P, -1),
        "cos": table(np.cos(ang), 1.0),
        "sin": table(np.sin(ang), sign),
    }
    arrays = {f"{k}_dram": np.ascontiguousarray(v) for k, v in arrays.items()}
    nc = _bacc.Bacc("TRN2", target_bir_lowering=False, num_devices=1)
    args = [nc.dram_tensor(k, v.shape, F32, kind="ExternalInput").ap() for k, v in arrays.items()]
    out = nc.dram_tensor("out_dram", (B * S, D), F32, kind="ExternalOutput").ap()
    adaln_block(nc, *args, out)
    r = _run(nc, [arrays], core_ids=[0])
    return r.results[0]["out_dram"].reshape(B, S, D)
```

```python
from contextlib import ExitStack

import numpy as np
import concourse.bass as bass
from concourse import mybir

B, S, D, H, HID = 2, 1024, 512, 16, 2048
DH = D // H
P = 128
NF = D // P
NI = S // P
NT = B * NI
HC = 256
NJ = HID // HC
NM = HC // P
TC = 512
NC = B * S // TC
TPC = TC // P
EPS = 1e-5
GATE_MIN = 0.25
MASKED = -3e38

F32, F32R, BF16 = mybir.dt.float32, mybir.dt.float32r, mybir.dt.bfloat16
ALU, ACT, AX = mybir.AluOpType, mybir.ActivationFunctionType, mybir.AxisListType

KB = 1024
R1, R2, R3, R4, R5 = 0, 64 * KB, 96 * KB, 128 * KB, 192 * KB

UNITS = B * H

MAX_PIECES = [(i, k0, min(TC, (i + 1) * P - k0)) for i in range(NI) for k0 in range(0, (i + 1) * P, TC)]
NMP = len(MAX_PIECES)
SPLIT_TILES = TC // P

EXP_PIECES = [[(0, 0, 512)], [(1, 128, 384), (3, 384, 128)], [(0, 512, 512)], [(2, 256, 256), (6, 768, 256)],
              [(1, 512, 512)], [(2, 512, 512)], [(3, 512, 512)], [(4, 512, 512)], [(5, 640, 384), (7, 896, 128)]]
assert sorted((k, q) for piece in EXP_PIECES for k, q0, n in piece for q in range(q0, q0 + n, P)
              ) == [(k, q * P) for k in range(NI) for q in range(k, NI)]
assert all(sum(n for _, _, n in piece) == TC for piece in EXP_PIECES)
HALF_DONE = ((3, 2), (8, 7))
NEP = len(EXP_PIECES)
NTB = 3
assert NEP % NTB == 0 and NMP % 2 == 0
AHEAD = 2
MAX_AT = [(0, 1), (2, 3), (4, 5), (6, 7, 8), (9, 10, 11), (), (), (), ()]
M_AT = 6
FILL_AT = {7: 0, 8: 1, 0: 2, 1: 3}
TURN_AT = 3
EVAC_AT = (5, 1)
FILL_ORDER = (0, 2, 1, 3)


def adaln_block(nc, x, c_t, wmod_a, wmod_b, wqkv, wo, wffn, cos, sin, out):
    ctx = ExitStack()
    with ctx:
        base = -(-nc.sbuf_base // 64) * 64

        def sb(name, n, dt, at):
            return nc.alloc_sbuf_tensor_at(name, [P, n], dt, offset=base + at)

        at = R5
        small = {}

        def keep(name, n, dt=F32):
            nonlocal at
            small[name] = sb(name, n, dt, at)
            at += (n * (2 if dt == BF16 else 4) + 31) // 32 * 32
            return small[name]

        ident = keep("ident", P)
        ident_r = keep("ident_r", P, F32R)
        ident_bf = keep("ident_bf", P, BF16)
        mask_bf = keep("mask_bf", P, BF16)
        mask_t_bf = keep("mask_t_bf", P, BF16)
        cos_sb = keep("cos_sb", 2 * NI * DH)
        sin_sb = keep("sin_sb", 2 * NI * DH)
        gates = keep("gates", 2 * B * D)
        modcol = keep("modcol", 4 * NF * B)
        gatecol = keep("gatecol", 2 * NF * B)
        gatesgn = keep("gatesgn", 2 * NF * B)
        c_sb = keep("c_sb", NF * B)
        silu_c = keep("silu_c", NF * B)
        eps_sb = keep("eps_sb", 1)
        stat6 = keep("stat6", 2 * 6)
        mv = keep("mv", 2 * 2)
        std = keep("std", 2)
        rstd = keep("rstd", 2)
        part0 = keep("part0", 2 * DH)
        negmax = keep("negmax", 2 * NI)
        negmax_b = keep("negmax_b", 2 * (NI - SPLIT_TILES))
        m_cols = keep("m_cols", 2 * NI * 2, F32R)
        rinv = keep("rinv", 2 * NI)
        assert base + at <= nc.sbuf_usable_end

        qk_raw = sb("qk_raw", H * 2 * NT * DH, F32, R1)
        wmod_a_sb = sb("wmod_a_sb", 4 * NF * D, F32, R1)
        wqkv_st = sb("wqkv_st", 3 * NF * D, F32, R1 + 32 * KB)
        v_raw = sb("v_raw", H * NT * DH, F32, R2)
        wmod_b_sb = sb("wmod_b_sb", 2 * NF * D, F32, R3)
        x_t = [sb(f"x_t{u}", D, F32, R3 + (16 + 2 * u) * KB) for u in range(2)]
        gate_rep = sb("gate_rep", 2 * NF * B * P, F32, R3 + 20 * KB)
        h1 = [sb(f"h1_{u}", D, F32, R3 + (28 + 2 * u) * KB) for u in range(2)]
        wqkv_hi = sb("wqkv_hi", 3 * NF * D, F32R, R4)
        wqkv_lo = sb("wqkv_lo", 3 * NF * D, F32R, R4 + 24 * KB)
        h1_hi = [sb(f"h1_hi{u}", D, F32R, R4 + (48 + 2 * u) * KB) for u in range(2)]
        h1_lo = [sb(f"h1_lo{u}", D, F32R, R4 + (52 + 2 * u) * KB) for u in range(2)]
        xn1 = [sb(f"xn1_{u}", D, F32, R4 + (56 + 2 * u) * KB) for u in range(2)]

        stack = [sb(f"stack{u}", 2 * NI * P, F32R, R4 + 8 * u * KB) for u in range(2)]
        qk_t = [sb(f"qk_t{u}", 2 * S, F32R, R4 + (16 + 8 * u) * KB) for u in range(2)]
        probs_t = [sb(f"probs_t{k}", TC, F32, R4 + (32 + 2 * k) * KB) for k in range(NTB)]
        VH = DH + 1
        v_head = [sb(f"v_head{u}", NI * VH, F32, R4 + (40 + 2 * u) * KB) for u in range(2)]
        o_cols = sb("o_cols", S, F32, R4 + 44 * KB)
        rope_a = sb("rope_a", 2 * NI * DH, F32, R4 + 50 * KB)
        rope_b = sb("rope_b", 2 * NI * DH, F32, R4 + 52 * KB)
        roped = sb("roped", 2 * NI * DH, F32, R4 + 54 * KB)
        wo_st = sb("wo_st", NF * D, F32, R4 + 56 * KB)
        o_all = sb("o_all", NT * D, F32, R3)

        wo_gated = sb("wo_gated", NF * D, F32, R1)
        o_tile = [sb(f"o_tile{u}", D, F32, R1 + (16 + 2 * u) * KB) for u in range(2)]
        o_hi = [sb(f"o_hi{u}", D, F32R, R1 + (20 + 2 * u) * KB) for u in range(2)]
        o_lo = [sb(f"o_lo{u}", D, F32R, R1 + (24 + 2 * u) * KB) for u in range(2)]
        xn2 = [sb(f"xn2_{u}", D, F32, R1 + (28 + 2 * u) * KB) for u in range(2)]
        h2 = [sb(f"h2_{u}", D, F32, R1 + (8 + 2 * u) * KB) for u in range(2)]
        wo_hi = [sb(f"wo_hi{b}", NF * D, F32R, R1 + (32 + 16 * b) * KB) for b in range(B)]
        wo_lo = [sb(f"wo_lo{b}", NF * D, F32R, R1 + (40 + 16 * b) * KB) for b in range(B)]
        x_res = sb("x_res", NT * D, F32, R2)
        h2_hi = sb("h2_hi", NF * B * S, F32R, R4)
        h2_lo = sb("h2_lo", NF * B * S, F32R, R4 + 32 * KB)

        GU, DN = 2 * NF * HC, NM * D
        w_gu_hi = [sb(f"w_gu_hi{v}", GU, F32R, R1 + 32 * v * KB) for v in range(2)]
        w_gu_lo = [sb(f"w_gu_lo{v}", GU, F32R, R1 + (32 * v + 8) * KB) for v in range(2)]
        w_dn_hi = [sb(f"w_dn_hi{v}", B * DN, F32R, R1 + (32 * v + 16) * KB) for v in range(2)]
        w_dn_lo = [sb(f"w_dn_lo{v}", B * DN, F32R, R1 + (32 * v + 24) * KB) for v in range(2)]
        wffn_st = sb("wffn_st", GU + DN, F32, R3)
        hidden = sb("hidden", NM * TC, F32, R3 + 12 * KB)
        hid_hi = [sb(f"hid_hi{v}", NM * TC, F32R, R3 + (16 + 8 * v) * KB) for v in range(2)]
        hid_lo = [sb(f"hid_lo{v}", NM * TC, F32R, R3 + (20 + 8 * v) * KB) for v in range(2)]
        dn_gated = sb("dn_gated", DN, F32, R5 + 1 * KB + 512)
        assert dn_gated.shape[1] * 4 <= 4 * KB

        wide = [ctx.enter_context(nc.psum_tensor(f"wide{k}", [P, 1024], F32)) for k in range(2)]
        bank = [ctx.enter_context(nc.psum_tensor(f"bank{k}", [P, 512], F32)) for k in range(4)]

        st_bank = [wide[0][:, 0:TC], wide[0][:, TC:2 * TC], wide[1][:, 0:TC]]
        turned = wide[1][:, TC:2 * TC]

        def sem(name):
            return ctx.enter_context(nc.semaphore(name))

        apart_marks = sem("apart_marks")
        consts = sem("consts")
        c_in, wmod_a_in, wmod_b_in = sem("c_in"), sem("wmod_a_in"), sem("wmod_b_in")
        wqkv_in, wo_in, rope_in = sem("wqkv_in"), sem("wo_in"), sem("rope_in")
        silu_done, mod_mm, mod_done = sem("silu_done"), sem("mod_mm"), sem("mod_done")
        gate_mm, gate_col, gate_rep_done, gate_bc, gate_done = sem("gate_mm"), sem("gate_col"), sem("gate_rep_done"), sem("gate_bc"), sem("gate_done")
        wqkv_hi_done, wqkv_lo_done = sem("wqkv_hi_done"), sem("wqkv_lo_done")
        x_in = [sem(f"x_in{u}") for u in range(2)]
        stats, aggr, std_done, rstd_done, xn_done = (sem(n) for n in ("stats", "aggr", "std_done", "rstd_done", "xn_done"))
        xn_t, h_done, hi_done, lo_done = (sem(n) for n in ("xn_t", "h_done", "hi_done", "lo_done"))
        q_mm, k_mm, v_mm = sem("q_mm"), sem("k_mm"), sem("v_mm")
        q_out, k_out, v_out = sem("q_out"), sem("k_out"), sem("v_out")
        rope_step, roped_done, stack_const, stack_hi, stack_done, v_staged = (
            sem(n) for n in ("rope_step", "roped_done", "stack_const", "stack_hi", "stack_done", "v_staged"))
        qk_filled, qk_emptied = sem("qk_filled"), sem("qk_emptied")
        scores, row_max, m_step, m_ready = sem("scores"), sem("row_max"), sem("m_step"), sem("m_ready")
        m_filled, m_emptied = sem("m_filled"), sem("m_emptied")
        scores_t, exp_done, pv_done = sem("scores_t"), sem("exp_done"), sem("pv_done")
        o_cols_out, o_turned = sem("o_cols_out"), sem("o_turned")
        rinv_done, head_out = sem("rinv_done"), sem("head_out")
        wo_step, wo_ready = sem("wo_step"), sem("wo_ready")
        xr_in = sem("xr_in")
        o_staged, o_t, o_hi_done, o_lo_done = sem("o_staged"), sem("o_t"), sem("o_hi_done"), sem("o_lo_done")
        attn_mm, res_done = sem("attn_mm"), sem("res_done")
        xn2_t, h2_done, h2_hi_done, h2_lo_done = sem("xn2_t"), sem("h2_done"), sem("h2_hi_done"), sem("h2_lo_done")
        wffn_in, wffn_read, w_gu_ready, w_dn_ready = sem("wffn_in"), sem("wffn_read"), sem("w_gu_ready"), sem("w_dn_ready")
        dn_mul, dn_split, dn_ready_0 = sem("dn_mul"), sem("dn_split"), sem("dn_ready_0")
        gu_split = sem("gu_split")
        gate_ps, up_ps, silu_ps, gated = sem("gate_ps"), sem("up_ps"), sem("silu_ps"), sem("gated")
        hid_hi_done, hid_lo_done, down_ps = sem("hid_hi_done"), sem("hid_lo_done"), sem("down_ps")
        stored = sem("stored")

        block = ctx.enter_context(nc.Block())

        def after(eng, semaphore, count):
            if isinstance(count, int) and count <= 0:
                return
            eng.wait_ge(semaphore, count)

        def apart(eng):
            eng.sem_inc(apart_marks, 1)

        x_rows = x.rearrange("(t p) d -> t p d", p=P)
        out_rows = out.rearrange("(c t p) d -> c p t d", p=P, t=TPC)

        def mod(kind, chunk, b):
            k = (kind * NF + chunk) * B + b
            return modcol[:, k:k + 1]

        SA, CA, SB, CB = range(4)

        @block.sync
        def _(sp):
            for u in range(B):
                sp.dma_start(x_t[u][:, :], x_rows[u * NI]).then_inc(x_in[u], 16)
            sp.dma_start(c_sb[:, :], c_t[:, :]).then_inc(c_in, 16)
            sp.dma_start(wmod_a_sb[:, :], wmod_a[:, :]).then_inc(wmod_a_in, 16)
            sp.dma_start(cos_sb[:, :], cos[:, :]).then_inc(rope_in, 16)
            sp.dma_start(sin_sb[:, :], sin[:, :]).then_inc(rope_in, 16)
            sp.dma_start(wmod_b_sb[:, :], wmod_b[:, :]).then_inc(wmod_b_in, 16)
            with sp.Fori(1, NI) as i:
                for u in range(B):
                    sp.wait_ge(xn_done, 2 * i + u - 1)
                    sp.dma_start(x_t[u][:, :], x[bass.ds((i + u * NI) * P, P), :]).then_inc(x_in[u], 16)
            sp.wait_ge(v_mm, NT)
            sp.dma_start(wo_st[:, :], wo[:, :]).then_inc(wo_in, 16)
            sp.wait_ge(v_staged, UNITS)
            for b in range(B):
                sp.dma_start(x_res[:, b * NI * D:(b + 1) * NI * D].rearrange("p (t d) -> p t d", d=D),
                             x[b * S:(b + 1) * S, :].rearrange("(t p) d -> p t d", p=P)).then_inc(xr_in, 16)
            sp.wait_ge(o_staged, NT)
            sp.dma_start(wffn_st[:, :], wffn[0:P, :]).then_inc(wffn_in, 16)
            with sp.Fori(1, NJ) as j:
                sp.wait_ge(wffn_read, j)
                sp.dma_start(wffn_st[:, :], wffn[bass.ds(j * P, P), :]).then_inc(wffn_in, 16)
            for c in range(NC):
                sp.wait_ge(res_done, NT + ((NJ - 1) * NC + c + 1) * TPC)
                sp.dma_start(out_rows[c],
                             x_res[:, c * TPC * D:(c + 1) * TPC * D].rearrange("p (t d) -> p t d", d=D)
                             ).then_inc(stored, 16)
            sp.wait_ge(stored, 16 * NC)

        @block.tensor
        def _(pe):
            def mod_columns(ps, w, kinds, done):
                for kk in range(kinds):
                    for ch in range(NF):
                        for f in range(NF):
                            o = (kk * NF + ch) * B
                            w0 = (kk * NF + f) * D + ch * P
                            last = nc.tensor.matmul(ps[:, o:o + B], w[:, w0:w0 + P], silu_c[:, f * B:(f + 1) * B],
                                                    start=(f == 0), stop=(f == NF - 1))
                last.then_inc(done, 1)

            pe.wait_ge(silu_done, 1)
            pe.wait_ge(wmod_a_in, 16)
            mod_columns(bank[3], wmod_a_sb, 4, mod_mm)

            def transpose_xn(i, u):
                pe.wait_ge(xn_done, 2 * i + u + 1)
                after(pe, h_done, 2 * i + u - 1)
                for f in range(NF):
                    last = nc.tensor.transpose(bank[u][:, f * P:(f + 1) * P], xn1[u][:, f * P:(f + 1) * P], ident[:, :])
                last.then_inc(xn_t, 1)

            def project(i, u):
                pe.wait_ge(hi_done, 2 * i + u + 1)
                pe.wait_ge(lo_done, 2 * i + u + 1)
                for w, (ps, done, read) in enumerate((
                        (wide[u][:, 0:512], q_mm, q_out),
                        (wide[u][:, 512:1024], k_mm, k_out),
                        (bank[2 + u][:, :], v_mm, v_out))):
                    after(pe, read, 2 * i + u - 1)
                    n = 0
                    for a, ww in ((h1_hi, wqkv_hi), (h1_hi, wqkv_lo), (h1_lo, wqkv_hi)):
                        for f in range(NF):
                            w0 = (w * NF + f) * D
                            last = nc.tensor.matmul(ps, a[u][:, f * P:(f + 1) * P], ww[:, w0:w0 + D],
                                                    start=(n == 0), stop=(n == 3 * NF - 1))
                            n += 1
                    last.then_inc(done, 1)

            pe.wait_ge(consts, 4)
            transpose_xn(0, 0)
            pe.wait_ge(wqkv_hi_done, 3)
            pe.wait_ge(wqkv_lo_done, 3)
            pe.wait_ge(mod_done, 1)
            def project_pair(i):
                transpose_xn(i, 1)
                project(i, 0)
                transpose_xn(i + 1, 0)
                project(i, 1)

            project_pair(0)
            with pe.Fori(1, NI - 1) as i:
                project_pair(i)
            transpose_xn(NI - 1, 1)
            project(NI - 1, 0)
            project(NI - 1, 1)

            pe.wait_ge(wmod_b_in, 16)
            pe.wait_ge(v_out, NT)
            mod_columns(bank[2], wmod_b_sb, 2, gate_mm)
            pe.wait_ge(q_out, NT)
            pe.wait_ge(k_out, NT)
            pe.wait_ge(gate_rep_done, 1)
            for g in range(2 * B):
                kind, b = divmod(g, B)
                for f in range(NF):
                    r = ((kind * NF + f) * B + b) * P
                    last = nc.tensor.transpose(wide[g // 2][:, (g % 2) * 512 + f * P:(g % 2) * 512 + (f + 1) * P],
                                               gate_rep[:, r:r + P], ident[:, :])
            last.then_inc(gate_bc, 1)

            def fill_stack(n, u, q):
                after(pe, stack_done, n + 1)
                if q == 0:
                    after(pe, m_emptied, 2 * n)
                else:
                    after(pe, qk_emptied, 4 * n + q)
                for t in range(4):
                    o = (FILL_ORDER[q] * 4 + t) * P
                    inst = nc.tensor.transpose(turned[:, t * P:(t + 1) * P].bitcast(F32R), stack[u][:, o:o + P],
                                               ident_r[:, :])
                inst.then_inc(qk_filled, 1)

            def score(n, u, j):
                i, k0, width = MAX_PIECES[j]
                after(pe, row_max, NMP * n + j - 1)
                if j == 0:
                    pe.wait_ge(qk_emptied, 4 * n + 2)
                if i == SPLIT_TILES and k0 == 0:
                    pe.wait_ge(qk_emptied, 4 * n + 4)
                diag = k0 + width == (i + 1) * P
                ps = bank[j % 2]
                inst = nc.tensor.matmul(ps[:, 0:width], qk_t[u][:, i * P:(i + 1) * P],
                                        qk_t[u][:, S + k0:S + k0 + width], start=True, stop=not diag)
                if diag:
                    inst = nc.tensor.matmul(ps[:, width - P:width], ident_bf[:, :], mask_bf[:, :], start=False, stop=True)
                inst.then_inc(scores, 1)

            def fill_maxima(n, u, half):
                if half == 0:
                    pe.wait_ge(m_ready, n + 1)
                    pe.wait_ge(qk_emptied, 4 * n + 4)
                    after(pe, head_out, n - 1)
                else:
                    pe.wait_ge(m_emptied, 2 * n + 1)
                for t in range(4):
                    c = (u * NI + half * 4 + t) * 2
                    inst = nc.tensor.matmul(turned[0:2, t * P:(t + 1) * P], m_cols[:, c:c + 2], ident_r[:, :],
                                            start=True, stop=True)
                inst.then_inc(m_filled, 1)

            def score_t(n, u, j):
                after(pe, exp_done, NEP * n + j - NTB + 1)
                if j == 0:
                    pe.wait_ge(m_emptied, 2 * n + 1)
                elif j == 2:
                    pe.wait_ge(m_emptied, 2 * n + 2)
                c = 0
                for kt, q0, width in EXP_PIECES[j]:
                    diag = q0 == kt * P
                    inst = nc.tensor.matmul(st_bank[j % NTB][:, c:c + width], qk_t[u][:, S + kt * P:S + (kt + 1) * P],
                                            qk_t[u][:, q0:q0 + width], start=True, stop=not diag)
                    if diag:
                        inst = nc.tensor.matmul(st_bank[j % NTB][:, c:c + P], ident_bf[:, :], mask_t_bf[:, :],
                                                start=False, stop=True)
                    c += width
                inst.then_inc(scores_t, 1)

            def weigh_values(n, u, j):
                pe.wait_ge(exp_done, NEP * n + j + 1)
                if j == 0:
                    pe.wait_ge(v_staged, n + 1)
                    after(pe, o_cols_out, 2 * n - 1)
                if j == 2:
                    after(pe, o_cols_out, 2 * n)
                c = 0
                for kt, q0, width in EXP_PIECES[j]:
                    half, q = divmod(q0, TC)
                    inst = nc.tensor.matmul(bank[2 + half][0:VH, q:q + width], v_head[u][:, kt * VH:(kt + 1) * VH],
                                            probs_t[j % NTB][:, c:c + width], start=width == TC and kt == 0,
                                            stop=(j, kt) == HALF_DONE[half])
                    c += width
                inst.then_inc(pv_done, 1)

            def turn_output(n, ahead):
                pe.wait_ge(o_cols_out, 2 * (n + 1))
                after(pe, head_out, n)
                if ahead >= 1:
                    pe.wait_ge(qk_emptied, 4 * (n + 2) + 4)
                for i in range(NI):
                    inst = nc.tensor.matmul(turned[:, i * VH:(i + 1) * VH], o_cols[0:VH, i * P:(i + 1) * P],
                                            ident[0:VH, 0:VH], start=True, stop=True)
                inst.then_inc(o_turned, 1)

            def unit(n, u, first, ahead):
                for s in range(NEP):
                    if s + AHEAD < NEP:
                        score_t(n, u, s + AHEAD)
                    elif ahead >= 1:
                        score_t(n + 1, 1 - u, s + AHEAD - NEP)
                    if s in FILL_AT:
                        q = FILL_AT[s]
                        if q >= 2 and ahead >= 1:
                            fill_stack(n + 1, 1 - u, q)
                        if q < 2 and ahead >= 2:
                            fill_stack(n + 2, u, q)
                    if s == TURN_AT and not first:
                        turn_output(n - 1, ahead)
                    if s == M_AT and ahead >= 1:
                        fill_maxima(n + 1, 1 - u, 0)
                    pieces = MAX_AT[s] if ahead >= 1 else ()
                    for j in pieces[:1]:
                        score(n + 1, 1 - u, j)
                    weigh_values(n, u, s)
                    for j in pieces[1:]:
                        score(n + 1, 1 - u, j)
                    if s == M_AT and ahead >= 1:
                        fill_maxima(n + 1, 1 - u, 1)

            pe.wait_ge(gate_done, 1)
            for q in range(4):
                fill_stack(0, 0, q)
            for j in range(NMP):
                score(0, 0, j)
            for half in range(2):
                fill_maxima(0, 0, half)
            for q in range(2):
                fill_stack(1, 1, q)
            for j in range(AHEAD):
                score_t(0, 0, j)
            for u in range(B):
                unit(u, u, u == 0, 2)
            with pe.Fori(1, H - 1) as h:
                for u in range(B):
                    unit(2 * h + u, u, False, 2)
            for u in range(B):
                unit(2 * (H - 1) + u, u, False, 1 - u)
            turn_output(UNITS - 1, 0)

            def transpose_o(i, u):
                pe.wait_ge(o_staged, 2 * i + u + 1)
                after(pe, o_lo_done, 2 * i + u - 1)
                for f in range(NF):
                    inst = nc.tensor.transpose(bank[u][:, f * P:(f + 1) * P], o_tile[u][:, f * P:(f + 1) * P], ident[:, :])
                inst.then_inc(o_t, 1)

            def project_out(i, u):
                pe.wait_ge(o_hi_done, 2 * i + u + 1)
                pe.wait_ge(o_lo_done, 2 * i + u + 1)
                after(pe, res_done, 2 * i + u - 1)
                n = 0
                for a, w in ((o_hi, wo_hi), (o_hi, wo_lo), (o_lo, wo_hi)):
                    for f in range(NF):
                        inst = nc.tensor.matmul(bank[2 + u][:, :], a[u][:, f * P:(f + 1) * P], w[u][:, f * D:(f + 1) * D],
                                                start=(n == 0), stop=(n == 3 * NF - 1))
                        n += 1
                inst.then_inc(attn_mm, 1)

            def transpose_xn2(i, u):
                pe.wait_ge(xn_done, NT + 2 * i + u + 1)
                after(pe, h2_done, 2 * i + u - 1)
                for f in range(NF):
                    inst = nc.tensor.transpose(wide[u][:, f * P:(f + 1) * P], xn2[u][:, f * P:(f + 1) * P], ident[:, :])
                inst.then_inc(xn2_t, 1)

            pe.wait_ge(head_out, UNITS)
            transpose_o(0, 0)
            pe.wait_ge(wo_ready, 2)
            transpose_o(0, 1)
            project_out(0, 0)
            def project_out_pair(i):
                transpose_o(i + 1, 0)
                project_out(i, 1)
                transpose_xn2(i, 0)
                transpose_o(i + 1, 1)
                project_out(i + 1, 0)
                transpose_xn2(i, 1)

            project_out_pair(0)
            with pe.Fori(1, NI - 1) as i:
                project_out_pair(i)
            project_out(NI - 1, 1)
            transpose_xn2(NI - 1, 0)
            transpose_xn2(NI - 1, 1)

            def gate_up(w, v, c):
                for m in range(NM):
                    for side, (ps, done, read) in enumerate(((wide[0], gate_ps, silu_ps), (wide[1], up_ps, gated))):
                        after(pe, read, NM * (w - 1) + m + 1)
                        n = 0
                        for ww, a in ((w_gu_hi, h2_hi), (w_gu_lo, h2_hi), (w_gu_hi, h2_lo)):
                            for f in range(NF):
                                w0 = (side * NF + f) * HC + m * P
                                a0 = f * B * S + c * TC
                                inst = nc.tensor.matmul(ps[:, m * TC:(m + 1) * TC], ww[v][:, w0:w0 + P], a[:, a0:a0 + TC],
                                                        start=(n == 0), stop=(n == 3 * NF - 1))
                                n += 1
                        inst.then_inc(done, 1)

            def down(w, v, c):
                b, p = c // (NC // B), c % 2
                pe.wait_ge(hid_hi_done, w + 1)
                pe.wait_ge(hid_lo_done, w + 1)
                for t in range(TPC):
                    pe.wait_ge(res_done, NT + TPC * (w - 1) + t + 1)
                    n = 0
                    for a, ww in ((hid_hi, w_dn_hi), (hid_hi, w_dn_lo), (hid_lo, w_dn_hi)):
                        for m in range(NM):
                            inst = nc.tensor.matmul(bank[t][:, :], a[p][:, m * TC + t * P:m * TC + (t + 1) * P],
                                                    ww[v][:, (b * NM + m) * D:(b * NM + m + 1) * D],
                                                    start=(n == 0), stop=(n == 3 * NM - 1))
                            n += 1
                    inst.then_inc(down_ps, 1)

            pe.wait_ge(h2_hi_done, NT)
            pe.wait_ge(h2_lo_done, NT)
            pe.wait_ge(res_done, NT)
            def slice_pair(jj, last):
                for n in range(2 * NC):
                    w, v, c = jj * 2 * NC + n, n // NC, n % NC
                    if not (last and n == 2 * NC - 1):
                        v1, c1 = (n + 1) // NC % 2, (n + 1) % NC
                        if c1 == 0:
                            pe.wait_ge(w_gu_ready, jj * 2 + v + 2)
                        gate_up(w + 1, v1, c1)
                    if c == 0:
                        pe.wait_ge(w_dn_ready, jj * 2 + v + 1)
                    down(w, v, c)

            pe.wait_ge(w_gu_ready, 1)
            gate_up(0, 0, 0)
            with pe.Fori(0, NJ // 2 - 1) as jj:
                slice_pair(jj, False)
            slice_pair(NJ // 2 - 1, True)

        @block.scalar
        def _(act):
            act.dma_start(wqkv_st[:, :], wqkv[:, :]).then_inc(wqkv_in, 16)
            act.wait_ge(c_in, 16)
            nc.scalar.activation(silu_c[:, :], c_sb[:, :], ACT.Silu).then_inc(silu_done, 1)

            def std_of(u, count):
                act.wait_ge(aggr, count)
                nc.scalar.activation(std[:, u:u + 1], mv[:, 2 * u + 1:2 * u + 2], ACT.Sqrt,
                                     bias=eps_sb[:, 0:1]).then_inc(std_done, 1)

            def modulate(i, u):
                act.wait_ge(xn_t, 2 * i + u + 1)
                after(act, lo_done, 2 * i + u - 1)
                after(act, v_mm, 2 * i + u - 1)
                for f in range(NF):
                    inst = nc.scalar.activation(h1[u][:, f * P:(f + 1) * P], bank[u][:, f * P:(f + 1) * P], ACT.Identity,
                                                bias=mod(SA, f, u), scale=mod(CA, f, u))
                inst.then_inc(h_done, 1)
                act.wait_ge(h_done, 2 * i + u + 1)
                nc.scalar.activation(h1_hi[u][:, :], h1[u][:, :], ACT.Copy).then_inc(hi_done, 1)

            def store_qk(i, u):
                o = (i + u * NI) * DH
                view = qk_raw[:, :].rearrange("p (h w n) -> p h w n", h=H, w=2)
                for which, (mm, done) in enumerate(((q_mm, q_out), (k_mm, k_out))):
                    act.wait_ge(mm, 2 * i + u + 1)
                    nc.scalar.activation(view[:, :, which, bass.ds(o, DH)],
                                         wide[u][:, which * 512:(which + 1) * 512].rearrange("p (h d) -> p h d", d=DH),
                                         ACT.Copy).then_inc(done, 1)

            act.wait_ge(consts, 4)
            std_of(0, 1)
            std_of(1, 2)
            act.wait_ge(wqkv_in, 16)
            for w in range(3):
                nc.scalar.activation(wqkv_hi[:, w * NF * D:(w + 1) * NF * D], wqkv_st[:, w * NF * D:(w + 1) * NF * D],
                                     ACT.Copy).then_inc(wqkv_hi_done, 1)
            act.wait_ge(mod_done, 1)
            modulate(0, 0)

            def pair1(i):
                std_of(0, 2 * i + 3)
                modulate(i, 1)
                store_qk(i, 0)
                std_of(1, 2 * i + 4)
                modulate(i + 1, 0)
                store_qk(i, 1)

            pair1(0)
            with act.Fori(1, NI - 1) as i:
                pair1(i)
            modulate(NI - 1, 1)
            store_qk(NI - 1, 0)
            store_qk(NI - 1, 1)

            def empty_stack(n, u, q):
                act.wait_ge(qk_filled, 4 * n + q + 1)
                nc.scalar.activation(qk_t[u][:, FILL_ORDER[q] * 512:(FILL_ORDER[q] + 1) * 512], turned, ACT.Copy
                                     ).then_inc(qk_emptied, 1)

            def empty_maxima(n, u, half):
                act.wait_ge(m_filled, 2 * n + half + 1)
                nc.scalar.activation(qk_t[u][0:2, half * 512:(half + 1) * 512], turned[0:2, :], ACT.Copy
                                     ).then_inc(m_emptied, 1)

            def exponentials(n, j):
                act.wait_ge(scores_t, NEP * n + j + 1)
                after(act, pv_done, NEP * n + j - NTB + 1)
                nc.scalar.activation(probs_t[j % NTB][:, :], st_bank[j % NTB], ACT.Exp).then_inc(exp_done, 1)

            def empty_output(n, half):
                act.wait_ge(pv_done, NEP * n + HALF_DONE[half][0] + 1)
                after(act, o_turned, n)
                nc.scalar.activation(o_cols[0:VH, half * TC:(half + 1) * TC], bank[2 + half][0:VH, :], ACT.Copy
                                     ).then_inc(o_cols_out, 1)

            def unit(n, u, first, ahead):
                for s in range(NEP):
                    if s + AHEAD < NEP:
                        exponentials(n, s + AHEAD)
                    elif ahead >= 1:
                        exponentials(n + 1, s + AHEAD - NEP)
                    if s in FILL_AT:
                        q = FILL_AT[s]
                        if q >= 2 and ahead >= 1:
                            empty_stack(n + 1, 1 - u, q)
                        if q < 2 and ahead >= 2:
                            empty_stack(n + 2, u, q)
                    if s == EVAC_AT[0]:
                        empty_output(n, 0)
                    if s == EVAC_AT[1] and not first:
                        empty_output(n - 1, 1)
                    if s == M_AT and ahead >= 1:
                        for half in range(2):
                            empty_maxima(n + 1, 1 - u, half)

            act.wait_ge(v_out, NT)
            for q in range(4):
                empty_stack(0, 0, q)
            for half in range(2):
                empty_maxima(0, 0, half)
            for q in range(2):
                empty_stack(1, 1, q)
            for j in range(AHEAD):
                exponentials(0, j)
            for u in range(B):
                unit(u, u, u == 0, 2)
            with act.Fori(1, H - 1) as h:
                for u in range(B):
                    unit(2 * h + u, u, False, 2)
            for u in range(B):
                unit(2 * (H - 1) + u, u, False, 1 - u)
            empty_output(UNITS - 1, 1)

            def high_o(i, u):
                act.wait_ge(o_t, 2 * i + u + 1)
                after(act, attn_mm, 2 * i + u - 1)
                nc.scalar.activation(o_hi[u][:, :], bank[u][:, :], ACT.Copy).then_inc(o_hi_done, 1)

            def modulate2(i, u):
                act.wait_ge(xn2_t, 2 * i + u + 1)
                after(act, h2_lo_done, 2 * i + u - 1)
                for f in range(NF):
                    inst = nc.scalar.activation(h2[u][:, f * P:(f + 1) * P], wide[u][:, f * P:(f + 1) * P], ACT.Identity,
                                                bias=mod(SB, f, u), scale=mod(CB, f, u))
                inst.then_inc(h2_done, 1)
                act.wait_ge(h2_done, 2 * i + u + 1)
                nc.scalar.activation(h2_hi[:, :].rearrange("p (f n) -> p f n", f=NF)[:, :, bass.ds((i + u * NI) * P, P)],
                                     h2[u][:, :].rearrange("p (f n) -> p f n", f=NF), ACT.Copy).then_inc(h2_hi_done, 1)

            act.wait_ge(head_out, UNITS)
            act.wait_ge(wo_ready, 2)
            high_o(0, 0)
            high_o(0, 1)
            def pair3(i):
                std_of(0, NT + 2 * i + 1)
                high_o(i + 1, 0)
                modulate2(i, 0)
                std_of(1, NT + 2 * i + 2)
                high_o(i + 1, 1)
                modulate2(i, 1)

            pair3(0)
            with act.Fori(1, NI - 1) as i:
                pair3(i)
            for u in range(2):
                std_of(u, NT + 2 * (NI - 1) + u + 1)
            for u in range(2):
                modulate2(NI - 1, u)

            def unit(w, p):
                for m in range(NM):
                    act.wait_ge(gate_ps, NM * w + m + 1)
                    after(act, hid_lo_done, w)
                    nc.scalar.activation(hidden[:, m * TC:(m + 1) * TC], wide[0][:, m * TC:(m + 1) * TC],
                                         ACT.Silu).then_inc(silu_ps, 1)
                act.wait_ge(gated, NM * (w + 1))
                after(act, down_ps, TPC * (w - 1))
                nc.scalar.activation(hid_hi[p][:, :], hidden[:, :], ACT.Copy).then_inc(hid_hi_done, 1)

            act.wait_ge(o_staged, NT)
            unit(0, 0)
            unit(1, 1)
            with act.Fori(1, NJ * NC // 2) as ww:
                unit(2 * ww, 0)
                unit(2 * ww + 1, 1)

        @block.vector
        def _(dve):
            def normalise(src, dst, u, count):
                apart(dve)
                nc.vector.bn_stats(stat6[:, 6 * u:6 * u + 6], src).then_inc(stats, 1)
                dve.wait_ge(stats, count)
                apart(dve)
                nc.vector.bn_aggr(mv[:, 2 * u:2 * u + 2], stat6[:, 6 * u:6 * u + 6]).then_inc(aggr, 1)
                dve.wait_ge(std_done, count)
                nc.vector.reciprocal(rstd[:, u:u + 1], std[:, u:u + 1]).then_inc(rstd_done, 1)
                dve.wait_ge(rstd_done, count)
                nc.vector.tensor_scalar(dst, src, mv[:, 2 * u:2 * u + 1], rstd[:, u:u + 1], ALU.subtract, ALU.mult
                                        ).then_inc(xn_done, 1)

            def norm1(i, u):
                dve.wait_ge(x_in[u], 16 * (i + 1))
                after(dve, xn_t, 2 * i + u - 1)
                normalise(x_t[u][:, :], xn1[u][:, :], u, 2 * i + u + 1)

            def store_v(i, u):
                dve.wait_ge(v_mm, 2 * i + u + 1)
                nc.vector.tensor_copy(v_raw[:, :].rearrange("p (h n) -> p h n", h=H)[:, :, bass.ds((i + u * NI) * DH, DH)],
                                      bank[2 + u][:, :].rearrange("p (h d) -> p h d", d=DH)).then_inc(v_out, 1)

            dve.wait_ge(consts, 4)
            norm1(0, 0)
            norm1(0, 1)
            dve.wait_ge(mod_mm, 1)
            one_plus = modcol[:, :].rearrange("p (k n) -> p k n", k=4)
            ps_kinds = bank[3][:, 0:4 * NF * B].rearrange("p (k n) -> p k n", k=4)
            for kind in range(4):
                inst = nc.vector.tensor_scalar(one_plus[:, kind], ps_kinds[:, kind], float(kind in (CA, CB)), None, ALU.add)
            inst.then_inc(mod_done, 1)
            for w in range(3):
                dve.wait_ge(wqkv_hi_done, w + 1)
                seg = slice(w * NF * D, (w + 1) * NF * D)
                nc.vector.tensor_tensor(wqkv_lo[:, seg], wqkv_st[:, seg], wqkv_hi[:, seg].bitcast(F32), ALU.subtract
                                        ).then_inc(wqkv_lo_done, 1)
            with dve.Fori(0, NI - 1) as i:
                norm1(i + 1, 0)
                store_v(i, 0)
                norm1(i + 1, 1)
                store_v(i, 1)
            store_v(NI - 1, 0)
            store_v(NI - 1, 1)

            dve.wait_ge(gate_mm, 1)
            gps = bank[2][:, 0:2 * NF * B]
            nc.vector.tensor_scalar(gatesgn[:, :], gps, 0.0, 2.0, ALU.is_ge, ALU.mult).then_inc(gate_col, 1)
            dve.wait_ge(gate_col, 1)
            nc.vector.tensor_scalar(gatesgn[:, :], gatesgn[:, :], -1.0, None, ALU.add).then_inc(gate_col, 1)
            dve.wait_ge(gate_col, 2)
            nc.vector.tensor_tensor(gatecol[:, :], gps, gatesgn[:, :], ALU.mult).then_inc(gate_col, 1)
            dve.wait_ge(gate_col, 3)
            nc.vector.tensor_scalar(gatecol[:, :], gatecol[:, :], GATE_MIN, None, ALU.max).then_inc(gate_col, 1)
            dve.wait_ge(gate_col, 4)
            nc.vector.tensor_tensor(gatecol[:, :], gatecol[:, :], gatesgn[:, :], ALU.mult).then_inc(gate_col, 1)
            dve.wait_ge(gate_col, 5)
            nc.vector.tensor_copy(gate_rep[:, :].rearrange("p (g r) -> p g r", r=P),
                                  gatecol[:, :].unsqueeze(2).broadcast_to([P, 2 * NF * B, P])).then_inc(gate_rep_done, 1)
            dve.wait_ge(gate_bc, 1)
            for g in range(2):
                inst = nc.vector.tensor_copy(gates[:, g * 1024:(g + 1) * 1024], wide[g][:, :])
            inst.then_inc(gate_done, 1)

            def maxima(n, u, j):
                i, k0, width = MAX_PIECES[j]
                dst = negmax[:, u * NI + i:u * NI + i + 1]
                if k0:
                    c = u * (NI - SPLIT_TILES) + i - SPLIT_TILES
                    dst = negmax_b[:, c:c + 1]
                dve.wait_ge(scores, NMP * n + j + 1)
                nc.vector.tensor_reduce(dst, bank[j % 2][:, 0:width], AX.X, ALU.max, negate=True).then_inc(row_max, 1)

            def split_maxima(n, u):
                dve.wait_ge(row_max, NMP * (n + 1))
                both = negmax[:, u * NI + SPLIT_TILES:(u + 1) * NI]
                nc.vector.tensor_tensor(both, both, negmax_b[:, u * SPLIT_TILES:(u + 1) * SPLIT_TILES], ALU.min
                                        ).then_inc(m_step, 1)
                m = negmax[:, u * NI:(u + 1) * NI]
                parts = m_cols[:, u * 2 * NI:(u + 1) * 2 * NI].rearrange("p (t s) -> p t s", s=2)
                dve.wait_ge(m_step, 2 * n + 1)
                after(dve, m_filled, 2 * (n - 1))
                nc.vector.tensor_copy(parts[:, :, 0], m).then_inc(m_step, 1)
                dve.wait_ge(m_step, 2 * n + 2)
                nc.vector.tensor_tensor(parts[:, :, 1], m, parts[:, :, 0].bitcast(F32), ALU.subtract).then_inc(m_ready, 1)

            def head_output(n, u, h):
                dve.wait_ge(o_turned, n + 1)
                ps = turned[:, 0:NI * VH].rearrange("p (i e) -> p i e", e=VH)
                after(dve, head_out, n)
                nc.vector.reciprocal(rinv[:, u * NI:(u + 1) * NI], ps[:, :, DH]).then_inc(rinv_done, 1)
                dve.wait_ge(rinv_done, n + 1)
                dst = o_all[:, u * NI * D:(u + 1) * NI * D].rearrange("p (i n) -> p i n", i=NI)[:, :, bass.ds(h * DH, DH)]
                nc.vector.tensor_tensor(dst, ps[:, :, 0:DH],
                                        rinv[:, u * NI:(u + 1) * NI].unsqueeze(2).broadcast_to([P, NI, DH]), ALU.mult
                                        ).then_inc(head_out, 1)

            def stack_high(n, u):
                dve.wait_ge(roped_done, n + 1)
                after(dve, qk_filled, 4 * (n - 1))
                st = stack[u][:, :].rearrange("p (w t s d) -> p w t s d", w=2, s=4, d=DH)
                src = roped[:, :].rearrange("p (w t d) -> p w t d", w=2, d=DH)
                for w, parts in enumerate((slice(1, 3), slice(1, 4, 2))):
                    inst = nc.vector.tensor_copy(st[:, w, :, parts], src[:, w].unsqueeze(2).broadcast_to([P, NI, 2, DH]))
                inst.then_inc(stack_hi, 1)

            def unit(n, u, h, first, ahead):
                for s in range(NEP):
                    if ahead >= 1:
                        for j in MAX_AT[s]:
                            maxima(n + 1, 1 - u, j)
                    if s == TURN_AT and not first:
                        head_output(n - 1, 1 - u, h - (1 - u))
                    if s == 2 and ahead >= 2:
                        stack_high(n + 2, u)
                if ahead >= 1:
                    split_maxima(n + 1, 1 - u)

            dve.wait_ge(v_mm, NT)
            for u in range(B):
                st = stack[u][:, :].rearrange("p (w t s d) -> p w t s d", w=2, s=4, d=DH)
                for w in range(2):
                    inst = nc.vector.tensor_copy(st[:, w, :, 0],
                                                 part0[:, w * DH:(w + 1) * DH].unsqueeze(1).broadcast_to([P, NI, DH]))
            inst.then_inc(stack_const, 1)
            stack_high(0, 0)
            stack_high(1, 1)
            for j in range(NMP):
                maxima(0, 0, j)
            split_maxima(0, 0)
            for u in range(B):
                unit(u, u, 0, u == 0, 2)
            with dve.Fori(1, H - 1) as h:
                for u in range(B):
                    unit(2 * h + u, u, h, False, 2)
            for u in range(B):
                unit(2 * (H - 1) + u, u, H - 1, False, 1 - u)
            head_output(UNITS - 1, 1, H - 1)

            def low_o(i, u):
                dve.wait_ge(o_hi_done, 2 * i + u + 1)
                after(dve, attn_mm, 2 * i + u - 1)
                nc.vector.tensor_tensor(o_lo[u][:, :], bank[u][:, :], o_hi[u][:, :].bitcast(F32), ALU.subtract
                                        ).then_inc(o_lo_done, 1)

            def residual(i, u):
                tile = x_res[:, bass.ds((i + u * NI) * D, D)]
                dve.wait_ge(attn_mm, 2 * i + u + 1)
                nc.vector.tensor_tensor(tile, bank[2 + u][:, :], tile, ALU.add).then_inc(res_done, 1)
                dve.wait_ge(res_done, 2 * i + u + 1)
                after(dve, xn2_t, 2 * i + u - 1)
                normalise(tile, xn2[u][:, :], u, NT + 2 * i + u + 1)

            dve.wait_ge(xr_in, 16 * B)
            low_o(0, 0)
            low_o(0, 1)
            def pair3(i):
                residual(i, 0)
                low_o(i + 1, 0)
                residual(i, 1)
                low_o(i + 1, 1)

            pair3(0)
            with dve.Fori(1, NI - 1) as i:
                pair3(i)
            for u in range(2):
                residual(NI - 1, u)

            def gate_hidden(w):
                for m in range(NM):
                    seg = slice(m * TC, (m + 1) * TC)
                    dve.wait_ge(up_ps, NM * w + m + 1)
                    dve.wait_ge(silu_ps, NM * w + m + 1)
                    nc.vector.tensor_tensor(hidden[:, seg], wide[1][:, seg], hidden[:, seg], ALU.mult).then_inc(gated, 1)

            def accumulate(w, c):
                for t in range(TPC):
                    tile = x_res[:, (c * TPC + t) * D:(c * TPC + t + 1) * D]
                    dve.wait_ge(down_ps, TPC * w + t + 1)
                    nc.vector.tensor_tensor(tile, bank[t][:, :], tile, ALU.add).then_inc(res_done, 1)

            def slice_pair(jj, last):
                for n in range(2 * NC):
                    w = jj * 2 * NC + n
                    if not (last and n == 2 * NC - 1):
                        gate_hidden(w + 1)
                    accumulate(w, n % NC)

            gate_hidden(0)
            with dve.Fori(0, NJ // 2 - 1) as jj:
                slice_pair(jj, False)
            slice_pair(NJ // 2 - 1, True)

        @block.gpsimd
        def _(pool):
            pool.memset(ident[:, :], 0.0).then_inc(consts, 1)
            pool.wait_ge(consts, 1)
            pool.affine_select(out=ident[:, :], in_=ident[:, :], compare_op=ALU.not_equal, fill=1.0,
                               base=0, pattern=[[-1, P]], channel_multiplier=1).then_inc(consts, 1)
            pool.memset(eps_sb[:, :], EPS)
            pool.memset(part0[:, :], 0.0)
            pool.memset(mask_t_bf[:, :], 0.0)
            pool.memset(mask_bf[:, :], 0.0).then_inc(consts, 1)
            pool.wait_ge(consts, 3)
            pool.memset(part0[:, DH:DH + 2], 1.0)
            pool.tensor_copy(ident_bf[:, :], ident[:, :])
            pool.tensor_copy(ident_r[:, :], ident[:, :])
            pool.affine_select(out=mask_t_bf[:, :], in_=mask_t_bf[:, :], compare_op=ALU.is_ge, fill=MASKED,
                               base=0, pattern=[[1, P]], channel_multiplier=-1)
            pool.affine_select(out=mask_bf[:, :], in_=mask_bf[:, :], compare_op=ALU.is_ge, fill=MASKED,
                               base=0, pattern=[[-1, P]], channel_multiplier=1).then_inc(consts, 1)

            def low_h(i, u):
                pool.wait_ge(hi_done, 2 * i + u + 1)
                after(pool, v_mm, 2 * i + u - 1)
                nc.gpsimd.tensor_tensor(h1_lo[u][:, :], h1[u][:, :], h1_hi[u][:, :].bitcast(F32), ALU.subtract
                                        ).then_inc(lo_done, 1)

            for u in range(2):
                low_h(0, u)
            with pool.Fori(1, NI) as i:
                for u in range(2):
                    low_h(i, u)

            def rotate(n, u, h):
                raw = qk_raw[:, bass.ds(h * 2 * NT * DH, 2 * NT * DH)].rearrange(
                    "p (w n) -> p w n", w=2)[:, :, u * NI * DH:(u + 1) * NI * DH]
                raw_pair = raw.rearrange("p w (n two) -> p w n two", two=2)
                tab, pair = "p (w n) -> p w n", "p (w n two) -> p w n two"
                after(pool, roped_done, n)
                pool.tensor_tensor(rope_a[:, :].rearrange(tab, w=2), raw, cos_sb[:, :].rearrange(tab, w=2), ALU.mult)
                for odd in range(2):
                    inst = pool.tensor_tensor(rope_b[:, :].rearrange(pair, w=2, two=2)[:, :, :, odd],
                                              raw_pair[:, :, :, 1 - odd],
                                              sin_sb[:, :].rearrange(pair, w=2, two=2)[:, :, :, odd], ALU.mult)
                inst.then_inc(rope_step, 1)
                pool.wait_ge(rope_step, n + 1)
                after(pool, stack_done, n)
                pool.tensor_tensor(roped[:, :], rope_a[:, :], rope_b[:, :], ALU.add).then_inc(roped_done, 1)

            def stage_v(n, u, h):
                after(pool, pv_done, NEP * (n - 1))
                apart(pool)
                pool.tensor_copy(v_head[u][:, :].rearrange("p (t e) -> p t e", e=VH)[:, :, 0:DH],
                                 v_raw[:, bass.ds(h * NT * DH + u * NI * DH, NI * DH)].rearrange("p (t d) -> p t d", d=DH)
                                 ).then_inc(v_staged, 1)

            def stack_low(n, u):
                pool.wait_ge(stack_hi, n + 1)
                st = stack[u][:, :].rearrange("p (w t s d) -> p w t s d", w=2, s=4, d=DH)
                src = roped[:, :].rearrange("p (w t d) -> p w t d", w=2, d=DH)
                for w, part in enumerate((3, 2)):
                    inst = pool.tensor_tensor(st[:, w, :, part], src[:, w], st[:, w, :, 1].bitcast(F32), ALU.subtract)
                inst.then_inc(stack_done, 1)

            def stage_unit(n, u, h, first):
                rotate(n, u, h)
                if not first:
                    stage_v(n - 1, 1 - u, h - (1 - u))
                stack_low(n, u)

            pool.wait_ge(rope_in, 32)
            pool.wait_ge(q_out, NT)
            pool.wait_ge(k_out, NT)
            pool.wait_ge(v_out, NT)
            for u in range(B):
                pool.memset(v_head[u][:, :].rearrange("p (t e) -> p t e", e=VH)[:, :, DH], 1.0)
            for u in range(B):
                stage_unit(u, u, 0, u == 0)
            with pool.Fori(1, H) as h:
                for u in range(B):
                    stage_unit(2 * h + u, u, h, False)
            stage_v(UNITS - 1, 1, H - 1)

            pool.wait_ge(wo_in, 16)
            pool.wait_ge(gate_done, 1)
            for b in range(B):
                g = gates[:, b * D:(b + 1) * D]
                after(pool, wo_ready, b)
                for f in range(NF):
                    seg = slice(f * D, (f + 1) * D)
                    inst = pool.tensor_tensor(wo_gated[:, seg], wo_st[:, seg], g, ALU.mult)
                inst.then_inc(wo_step, 1)
                pool.wait_ge(wo_step, 2 * b + 1)
                pool.tensor_copy(wo_hi[b][:, :], wo_gated[:, :]).then_inc(wo_step, 1)
                pool.wait_ge(wo_step, 2 * b + 2)
                pool.tensor_tensor(wo_lo[b][:, :], wo_gated[:, :], wo_hi[b][:, :].bitcast(F32), ALU.subtract
                                   ).then_inc(wo_ready, 1)

            def stage_o(i, u):
                after(pool, o_t, 2 * i + u - 1)
                apart(pool)
                pool.tensor_copy(o_tile[u][:, :], o_all[:, bass.ds((i + u * NI) * D, D)]).then_inc(o_staged, 1)

            def low_h2(i, u):
                pool.wait_ge(h2_hi_done, 2 * i + u + 1)
                seg = bass.ds((i + u * NI) * P, P)
                hi = h2_hi[:, :].rearrange("p (f n) -> p f n", f=NF)[:, :, seg]
                lo = h2_lo[:, :].rearrange("p (f n) -> p f n", f=NF)[:, :, seg]
                pool.tensor_tensor(lo, h2[u][:, :].rearrange("p (f n) -> p f n", f=NF), hi.bitcast(F32), ALU.subtract
                                   ).then_inc(h2_lo_done, 1)

            pool.wait_ge(head_out, UNITS)
            stage_o(0, 0)
            stage_o(0, 1)
            with pool.Fori(0, NI - 1) as i:
                for u in range(2):
                    stage_o(i + 1, u)
                for u in range(2):
                    low_h2(i, u)
            for u in range(2):
                low_h2(NI - 1, u)

            def stage_slice(j, v, part):
                gu = wffn_st[:, 0:GU]
                if part == 0:
                    pool.wait_ge(wffn_in, 16 * (j + 1))
                    after(pool, down_ps, (j - 1) * NC * TPC)
                    apart(pool)
                    pool.tensor_copy(w_gu_hi[v][:, :], gu).then_inc(gu_split, 1)
                elif part == 1:
                    pool.wait_ge(gu_split, j + 1)
                    pool.tensor_tensor(w_gu_lo[v][:, :], gu, w_gu_hi[v][:, :].bitcast(F32), ALU.subtract
                                       ).then_inc(w_gu_ready, 1)
                else:
                    b = part - 2
                    g = gates[:, (B + b) * D:(B + b + 1) * D]
                    seg = slice(b * DN, (b + 1) * DN)
                    if b == 1:
                        pool.wait_ge(dn_ready_0, j + 1)
                    multiplied, split = ((dn_mul, dn_ready_0), (wffn_read, w_dn_ready))[b]
                    for m in range(NM):
                        inst = pool.tensor_tensor(dn_gated[:, m * D:(m + 1) * D],
                                                  wffn_st[:, GU + m * D:GU + (m + 1) * D], g, ALU.mult)
                    inst.then_inc(multiplied, 1)
                    pool.wait_ge(multiplied, j + 1)
                    apart(pool)
                    pool.tensor_copy(w_dn_hi[v][:, seg], dn_gated[:, :]).then_inc(dn_split, 1)
                    pool.wait_ge(dn_split, 2 * j + b + 1)
                    pool.tensor_tensor(w_dn_lo[v][:, seg], dn_gated[:, :], w_dn_hi[v][:, seg].bitcast(F32), ALU.subtract
                                       ).then_inc(split, 1)

            def low_hidden(w, p):
                pool.wait_ge(hid_hi_done, w + 1)
                after(pool, down_ps, TPC * (w - 1))
                pool.tensor_tensor(hid_lo[p][:, :], hidden[:, :], hid_hi[p][:, :].bitcast(F32), ALU.subtract
                                   ).then_inc(hid_lo_done, 1)

            def slice_units(j, stage_v):
                for c in range(NC):
                    low_hidden(j * NC + c, c % 2)
                    if stage_v is not None:
                        stage_slice(j + 1, stage_v, c)

            pool.wait_ge(h2_hi_done, NT)
            for part in range(4):
                stage_slice(0, 0, part)
            slice_units(0, 1)
            with pool.Fori(0, NJ // 2 - 1) as jj:
                slice_units(2 * jj + 1, 0)
                slice_units(2 * jj + 2, 1)
            slice_units(NJ - 1, None)


def kernel(L0_attn_x, L0_attn_wq, L0_attn_wk, L0_attn_wv, L0_attn_wo, L0_ffn_w_gate, L0_ffn_w_up, L0_ffn_w_down,
           L0_c, L0_wmod):
    import concourse.bacc as _bacc
    from concourse.bass_utils import run_bass_kernel_spmd as _run

    def rows(w):
        w = np.asarray(w)
        return w.reshape(w.shape[0] // P, P, w.shape[1]).transpose(1, 0, 2)

    wq, wk, wv, wo = (rows(np.asarray(w).T) for w in (L0_attn_wq, L0_attn_wk, L0_attn_wv, L0_attn_wo))
    wmod = np.asarray(L0_wmod).reshape(NF, P, 6, D).transpose(1, 2, 0, 3)
    sides = [np.asarray(w).T.reshape(NF, P, NJ, HC).transpose(2, 1, 0, 3).reshape(NJ, P, NF * HC)
             for w in (L0_ffn_w_gate, L0_ffn_w_up)]
    down = np.asarray(L0_ffn_w_down).T.reshape(NJ, NM, P, D).transpose(0, 2, 1, 3).reshape(NJ, P, NM * D)

    inv_freq = np.float32(10000.0) ** (np.float32(-2.0) * np.arange(DH // 2, dtype=np.float32) / np.float32(DH))
    ang = (np.arange(S, dtype=np.float32)[:, None] * inv_freq[None, :]).astype(np.float32)
    scale = np.array([1.0 / np.sqrt(np.float32(DH)), 1.0], np.float32)
    sign = np.tile(np.array([-1.0, 1.0], np.float32), DH // 2)

    def table(t, s):
        t = (np.repeat(t, 2, axis=-1) * s).astype(np.float32)
        t = scale[:, None, None] * t[None]
        return t.reshape(2, NI, P, DH).transpose(2, 0, 1, 3).reshape(P, 2 * NI * DH)

    arrays = {
        "x": np.asarray(L0_attn_x).reshape(B * S, D),
        "c_t": np.asarray(L0_c).T.reshape(NF, P, B).transpose(1, 0, 2).reshape(P, NF * B),
        "wmod_a": wmod[:, [0, 1, 3, 4]].reshape(P, -1),
        "wmod_b": wmod[:, [2, 5]].reshape(P, -1),
        "wqkv": np.stack([wq, wk, wv], 1).reshape(P, -1),
        "wo": wo.reshape(P, -1),
        "wffn": np.concatenate([*sides, down], axis=2).reshape(NJ * P, -1),
        "cos": table(np.cos(ang), 1.0),
        "sin": table(np.sin(ang), sign),
    }
    arrays = {f"{k}_dram": np.ascontiguousarray(v) for k, v in arrays.items()}
    nc = _bacc.Bacc("TRN2", target_bir_lowering=False, num_devices=1)
    args = [nc.dram_tensor(k, v.shape, F32, kind="ExternalInput").ap() for k, v in arrays.items()]
    out = nc.dram_tensor("out_dram", (B * S, D), F32, kind="ExternalOutput").ap()
    adaln_block(nc, *args, out)
    r = _run(nc, [arrays], core_ids=[0])
    return r.results[0]["out_dram"].reshape(B, S, D)
```

```python
from contextlib import ExitStack

import numpy as np
import concourse.bass as bass
from concourse import mybir

B, S, D, H, HID = 2, 1024, 512, 16, 2048
DH = D // H
P = 128
NF = D // P
NI = S // P
NT = B * NI
HC = 256
NJ = HID // HC
NM = HC // P
TC = 512
NC = B * S // TC
TPC = TC // P
EPS = 1e-5
GATE_MIN = 0.25
MASKED = -3e38

F32, F32R, BF16 = mybir.dt.float32, mybir.dt.float32r, mybir.dt.bfloat16
ALU, ACT, AX = mybir.AluOpType, mybir.ActivationFunctionType, mybir.AxisListType

KB = 1024
R1, R2, R3, R4, R5 = 0, 64 * KB, 96 * KB, 128 * KB, 192 * KB + 128

UNITS = B * H

MAX_PIECES = [(i, k0, min(TC, (i + 1) * P - k0)) for i in range(NI) for k0 in range(0, (i + 1) * P, TC)]
NMP = len(MAX_PIECES)
SPLIT_TILES = TC // P

EXP_PIECES = [[(0, 0, 512)], [(1, 128, 384), (3, 384, 128)], [(0, 512, 512)], [(2, 256, 256), (6, 768, 256)],
              [(1, 512, 512)], [(2, 512, 512)], [(3, 512, 512)], [(4, 512, 512)], [(5, 640, 384), (7, 896, 128)]]
assert sorted((k, q) for piece in EXP_PIECES for k, q0, n in piece for q in range(q0, q0 + n, P)
              ) == [(k, q * P) for k in range(NI) for q in range(k, NI)]
assert all(sum(n for _, _, n in piece) == TC for piece in EXP_PIECES)
HALF_DONE = ((3, 2), (8, 7))
NEP = len(EXP_PIECES)
NTB = 3
assert NEP % NTB == 0 and NMP % 2 == 0
AHEAD = 3
LATE = 5
BEFORE = {7: [("fill", 1)], 8: [("fill", 2)], 0: [("fill", 3)], 1: [("m", 0)], 3: [("turn", 0)], 4: [("turn", 1)]}
AFTER = {5: [("fill", 0)], 6: [("m", 1)]}
FILL_ORDER = (0, 2, 1, 3)
MAX_AT = {7: (0, 1), 8: (2, 3), 0: (4, 5), 1: (6, 7), 2: (8,), 3: (9, 10), 4: (11,)}
M_PIECES = (4, NMP)
SPLIT_AT = (0, 5)
M_AT = 7
HIGH_AT = 7
OUT_AT = 5
EVAC_AT = (5, 1)


def adaln_block(nc, x, c_t, wmod_a, wmod_b, wqkv, wo, wffn, cos, sin, out):
    ctx = ExitStack()
    with ctx:
        base = -(-nc.sbuf_base // 64) * 64

        def sb(name, n, dt, at):
            return nc.alloc_sbuf_tensor_at(name, [P, n], dt, offset=base + at)

        at = R5

        def keep(name, n, dt=F32):
            nonlocal at
            tensor = sb(name, n, dt, at)
            at += (n * (2 if dt == BF16 else 4) + 31) // 32 * 32
            return tensor

        ident = keep("ident", P)
        ident_r = keep("ident_r", P, F32R)
        ident_bf = keep("ident_bf", P, BF16)
        mask_bf = keep("mask_bf", P, BF16)
        tables_at = at
        cos_sb = keep("cos_sb", 2 * NI * DH)
        sin_sb = keep("sin_sb", 2 * NI * DH)
        mask_t_bf = keep("mask_t_bf", P, BF16)
        gates_at = at
        gates = keep("gates", 2 * B * D)
        modcol = keep("modcol", 4 * NF * B)
        gatecol = keep("gatecol", 2 * NF * B)
        gatesgn = keep("gatesgn", 2 * NF * B)
        c_sb = keep("c_sb", NF * B)
        silu_c = keep("silu_c", NF * B)
        eps_sb = keep("eps_sb", 1)
        stat6 = keep("stat6", 2 * 6)
        mv = keep("mv", 2 * 2)
        std = keep("std", 2)
        rstd = keep("rstd", 2)
        part0 = keep("part0", 2 * DH)
        negmax = keep("negmax", 2 * NI)
        negmax_b = keep("negmax_b", 2 * (NI - SPLIT_TILES))
        ones = keep("ones", NI)
        fold = keep("fold", DH + 1)
        m_cols = keep("m_cols", 2 * NI * 2, F32R)
        rinv = keep("rinv", 2 * NI)
        assert base + at <= nc.sbuf_usable_end

        qk_raw = sb("qk_raw", H * 2 * NT * DH, F32, R1)
        wmod_a_sb = sb("wmod_a_sb", 2 * NF * D, F32, R1)
        wqkv_st = sb("wqkv_st", 3 * NF * D, F32, R1 + 32 * KB)
        v_raw = sb("v_raw", H * NT * DH, F32, R2)
        wmod_b_sb = sb("wmod_b_sb", 4 * NF * D, F32, R3)
        x_t = [sb(f"x_t{u}", D, F32, R4 + (60 + 2 * u) * KB) for u in range(2)]
        gate_rep = sb("gate_rep", 2 * NF * B * P, F32, R4 + 32 * KB)
        h1 = [sb(f"h1_{u}", D, F32, gates_at + 2 * u * KB) for u in range(2)]
        wqkv_hi = sb("wqkv_hi", 3 * NF * D, F32R, R4)
        wqkv_lo = sb("wqkv_lo", 3 * NF * D, F32R, R4 + 24 * KB)
        h1_hi = [sb(f"h1_hi{u}", D, F32R, R4 + (48 + 2 * u) * KB) for u in range(2)]
        h1_lo = [sb(f"h1_lo{u}", D, F32R, R4 + (52 + 2 * u) * KB) for u in range(2)]
        xn1 = [sb(f"xn1_{u}", D, F32, R4 + (56 + 2 * u) * KB) for u in range(2)]

        stack = [sb(f"stack{u}", 2 * NI * P, F32R, R4 + 8 * u * KB) for u in range(2)]
        qk_t = [sb(f"qk_t{u}", 2 * S, F32R, R4 + (16 + 8 * u) * KB) for u in range(2)]
        probs_t = [sb(f"probs_t{k}", TC, F32, R4 + (32 + 2 * k) * KB) for k in range(NTB)]
        probs_hi = [sb(f"probs_hi{k}", TC, F32R, R4 + (38 + 2 * k) * KB) for k in range(NTB)]
        probs_lo = [sb(f"probs_lo{k}", TC, F32R, R4 + (44 + 2 * k) * KB) for k in range(NTB)]
        VH = 2 * DH + 1
        VB = (NI * VH * 4 + 31) // 32 * 32
        o_cols = sb("o_cols", S, F32, R4 + 50 * KB)
        v_head = [sb(f"v_head{u}", NI * VH, F32R, R4 + 54 * KB + u * VB) for u in range(2)]
        rope_at = R4 + 54 * KB + 2 * VB
        assert rope_at + 6 * KB <= R5
        rope_a = sb("rope_a", 2 * NI * DH, F32, rope_at)
        rope_b = sb("rope_b", 2 * NI * DH, F32, rope_at + 2 * KB)
        roped = sb("roped", 2 * NI * DH, F32, rope_at + 4 * KB)
        wo_st = sb("wo_st", NF * D, F32, R4)
        o_all = sb("o_all", NT * D, F32, R3)

        wo_gated = sb("wo_gated", NF * D, F32, R1 + 8 * KB)
        o_tile = [sb(f"o_tile{u}", D, F32, R1 + (16 + 2 * u) * KB) for u in range(2)]
        o_hi = [sb(f"o_hi{u}", D, F32R, R1 + (20 + 2 * u) * KB) for u in range(2)]
        o_lo = [sb(f"o_lo{u}", D, F32R, R1 + (24 + 2 * u) * KB) for u in range(2)]
        xn2 = [sb(f"xn2_{u}", D, F32, R1 + (28 + 2 * u) * KB) for u in range(2)]
        h2 = [sb(f"h2_{u}", D, F32, tables_at + 2 * u * KB) for u in range(2)]
        wo_hi = [sb(f"wo_hi{b}", NF * D, F32R, R1 + (32 + 16 * b) * KB) for b in range(B)]
        wo_lo = [sb(f"wo_lo{b}", NF * D, F32R, R1 + (40 + 16 * b) * KB) for b in range(B)]
        x_res = sb("x_res", NT * D, F32, R2)
        h2_hi = sb("h2_hi", NF * B * S, F32R, R4)
        h2_lo = sb("h2_lo", NF * B * S, F32R, R4 + 32 * KB)

        GU, DN = 2 * NF * HC, NM * D
        w_gu_hi = [sb(f"w_gu_hi{v}", GU, F32R, R1 + 32 * v * KB) for v in range(2)]
        w_gu_lo = [sb(f"w_gu_lo{v}", GU, F32R, R1 + (32 * v + 8) * KB) for v in range(2)]
        w_dn_hi = [sb(f"w_dn_hi{v}", B * DN, F32R, R1 + (32 * v + 16) * KB) for v in range(2)]
        w_dn_lo = [sb(f"w_dn_lo{v}", B * DN, F32R, R1 + (32 * v + 24) * KB) for v in range(2)]
        wffn_st = sb("wffn_st", GU + DN, F32, R3)
        hidden = sb("hidden", NM * TC, F32, R3 + 12 * KB)
        hid_hi = [sb(f"hid_hi{v}", NM * TC, F32R, R3 + (16 + 8 * v) * KB) for v in range(2)]
        hid_lo = [sb(f"hid_lo{v}", NM * TC, F32R, R3 + (20 + 8 * v) * KB) for v in range(2)]
        dn_gated = sb("dn_gated", DN, F32, tables_at)
        assert dn_gated.shape[1] * 4 <= 4 * KB

        wide = [ctx.enter_context(nc.psum_tensor(f"wide{k}", [P, 1024], F32)) for k in range(2)]
        bank = [ctx.enter_context(nc.psum_tensor(f"bank{k}", [P, 512], F32)) for k in range(4)]

        st_bank = [wide[0][:, 0:TC], wide[0][:, TC:2 * TC], wide[1][:, 0:TC]]
        turned = wide[1][:, TC:2 * TC]

        def sem(name):
            return ctx.enter_context(nc.semaphore(name))

        apart_marks = sem("apart_marks")
        consts = sem("consts")
        c_in, wmod_a_in, wmod_b_in = sem("c_in"), sem("wmod_a_in"), sem("wmod_b_in")
        wo_in, rope_in = sem("wo_in"), sem("rope_in")
        wqkv_in = [sem(f"wqkv_in{w}") for w in range(3)]
        silu_done, mod_mm, mod_done = sem("silu_done"), sem("mod_mm"), sem("mod_done")
        gate_mm, gate_col, gate_rep_done, gate_bc, gate_done = (
            sem(n) for n in ("gate_mm", "gate_col", "gate_rep_done", "gate_bc", "gate_done"))
        wqkv_hi_done, wqkv_lo_done = sem("wqkv_hi_done"), sem("wqkv_lo_done")
        x_in = [sem(f"x_in{u}") for u in range(2)]
        stats, aggr, std_done, rstd_done, xn_done = (sem(n) for n in ("stats", "aggr", "std_done", "rstd_done", "xn_done"))
        xn_t, h_done, hi_done, lo_done = (sem(n) for n in ("xn_t", "h_done", "hi_done", "lo_done"))
        q_mm, k_mm, v_mm = sem("q_mm"), sem("k_mm"), sem("v_mm")
        q_out, k_out, v_out = sem("q_out"), sem("k_out"), sem("v_out")
        rope_step, roped_done, stack_const, stack_hi, stack_done, v_staged = (
            sem(n) for n in ("rope_step", "roped_done", "stack_const", "stack_hi", "stack_done", "v_staged"))
        qk_filled, qk_emptied = sem("qk_filled"), sem("qk_emptied")
        scores, row_max, m_step, m_ready = sem("scores"), sem("row_max"), sem("m_step"), sem("m_ready")
        m_filled, m_emptied = sem("m_filled"), sem("m_emptied")
        scores_t, exp_done, exp_split = sem("scores_t"), sem("exp_done"), sem("exp_split")
        pv_hi_done, pv_done = sem("pv_hi_done"), sem("pv_done")
        v_hi_done = sem("v_hi_done")
        o_cols_out, o_turned = sem("o_cols_out"), sem("o_turned")
        rinv_done, head_out = sem("rinv_done"), sem("head_out")
        wo_step, wo_ready = sem("wo_step"), sem("wo_ready")
        xr_in = sem("xr_in")
        o_staged, o_t, o_hi_done, o_lo_done = sem("o_staged"), sem("o_t"), sem("o_hi_done"), sem("o_lo_done")
        attn_mm, res_done = sem("attn_mm"), sem("res_done")
        xn2_t, h2_done, h2_hi_done, h2_lo_done = sem("xn2_t"), sem("h2_done"), sem("h2_hi_done"), sem("h2_lo_done")
        wffn_in, wffn_read, w_gu_ready, w_dn_ready = sem("wffn_in"), sem("wffn_read"), sem("w_gu_ready"), sem("w_dn_ready")
        dn_mul, dn_split, dn_ready_0 = sem("dn_mul"), sem("dn_split"), sem("dn_ready_0")
        gu_split = sem("gu_split")
        gate_ps, up_ps, silu_ps, gated = sem("gate_ps"), sem("up_ps"), sem("silu_ps"), sem("gated")
        hid_hi_done, hid_lo_done, down_ps = sem("hid_hi_done"), sem("hid_lo_done"), sem("down_ps")
        stored = sem("stored")

        block = ctx.enter_context(nc.Block())

        def after(eng, semaphore, count):
            if isinstance(count, int) and count <= 0:
                return
            eng.wait_ge(semaphore, count)

        def apart(eng):
            eng.sem_inc(apart_marks, 1)

        x_rows = x.rearrange("(t p) d -> t p d", p=P)
        out_rows = out.rearrange("(c t p) d -> c p t d", p=P, t=TPC)

        def mod(kind, chunk, b):
            k = (kind * NF + chunk) * B + b
            return modcol[:, k:k + 1]

        SA, CA, SB, CB = range(4)

        @block.sync
        def _(sp):
            sp.dma_start(c_sb[:, :], c_t[:, :]).then_inc(c_in, 16)
            for u in range(B):
                sp.dma_start(x_t[u][:, :], x_rows[u * NI]).then_inc(x_in[u], 16)
            sp.dma_start(wmod_a_sb[:, :], wmod_a[:, :]).then_inc(wmod_a_in, 16)
            for w in range(3):
                seg = slice(w * NF * D, (w + 1) * NF * D)
                sp.dma_start(wqkv_st[:, seg], wqkv[:, seg]).then_inc(wqkv_in[w], 16)
            sp.dma_start(cos_sb[:, :], cos[:, :]).then_inc(rope_in, 16)
            sp.dma_start(sin_sb[:, :], sin[:, :]).then_inc(rope_in, 16)
            for u in range(B):
                sp.wait_ge(xn_done, u + 1)
                sp.dma_start(x_t[u][:, :], x_rows[1 + u * NI]).then_inc(x_in[u], 16)
            sp.dma_start(wmod_b_sb[:, :], wmod_b[:, :]).then_inc(wmod_b_in, 16)
            with sp.Fori(2, NI) as i:
                for u in range(B):
                    sp.wait_ge(xn_done, 2 * i + u - 1)
                    sp.dma_start(x_t[u][:, :], x[bass.ds((i + u * NI) * P, P), :]).then_inc(x_in[u], 16)
            sp.wait_ge(qk_filled, 4 * (UNITS - 1))
            sp.dma_start(wo_st[:, :], wo[:, :]).then_inc(wo_in, 16)
            sp.wait_ge(v_staged, UNITS)
            for b in range(B):
                sp.dma_start(x_res[:, b * NI * D:(b + 1) * NI * D].rearrange("p (t d) -> p t d", d=D),
                             x[b * S:(b + 1) * S, :].rearrange("(t p) d -> p t d", p=P)).then_inc(xr_in, 16)
            sp.wait_ge(o_staged, 2 * -(-(GU + DN) // D))
            sp.dma_start(wffn_st[:, :], wffn[0:P, :]).then_inc(wffn_in, 16)
            with sp.Fori(1, NJ) as j:
                sp.wait_ge(wffn_read, j)
                sp.wait_ge(w_gu_ready, j)
                sp.dma_start(wffn_st[:, :], wffn[bass.ds(j * P, P), :]).then_inc(wffn_in, 16)
            for c in range(NC):
                sp.wait_ge(res_done, NT + ((NJ - 1) * NC + c + 1) * TPC)
                sp.dma_start(out_rows[c],
                             x_res[:, c * TPC * D:(c + 1) * TPC * D].rearrange("p (t d) -> p t d", d=D)
                             ).then_inc(stored, 16)
            sp.wait_ge(stored, 16 * NC)

        @block.tensor
        def _(pe):
            def mod_column(ps, w, kk, ch):
                o = (kk * NF + ch) * B
                for f in range(NF):
                    w0 = (kk * NF + f) * D + ch * P
                    inst = nc.tensor.matmul(ps[:, o:o + B], w[:, w0:w0 + P], silu_c[:, f * B:(f + 1) * B],
                                            start=(f == 0), stop=(f == NF - 1))
                return inst

            pe.wait_ge(silu_done, 1)
            pe.wait_ge(wmod_a_in, 16)
            for kk in range(2):
                for ch in range(NF):
                    inst = mod_column(bank[3], wmod_a_sb, kk, ch)
            inst.then_inc(mod_mm, 1)

            def transpose_xn(i, u):
                pe.wait_ge(xn_done, 2 * i + u + 1)
                after(pe, h_done, 2 * i + u - 1)
                for f in range(NF):
                    last = nc.tensor.transpose(bank[u][:, f * P:(f + 1) * P], xn1[u][:, f * P:(f + 1) * P], ident[:, :])
                last.then_inc(xn_t, 1)

            columns = [(kk, ch) for kk in range(4) for ch in range(NF)]

            def project(i, u, with_columns=False):
                pe.wait_ge(hi_done, 2 * i + u + 1)
                pe.wait_ge(lo_done, 2 * i + u + 1)
                for w, (ps, done, read) in enumerate((
                        (wide[u][:, 0:512], q_mm, q_out),
                        (wide[u][:, 512:1024], k_mm, k_out),
                        (bank[2 + u][:, :], v_mm, v_out))):
                    after(pe, read, 2 * i + u - 1)
                    n = 0
                    for a, ww in ((h1_hi, wqkv_hi), (h1_hi, wqkv_lo), (h1_lo, wqkv_hi)):
                        for f in range(NF):
                            w0 = (w * NF + f) * D
                            last = nc.tensor.matmul(ps, a[u][:, f * P:(f + 1) * P], ww[:, w0:w0 + D],
                                                    start=(n == 0), stop=(n == 3 * NF - 1))
                            n += 1
                        if with_columns and columns:
                            kk, ch = columns.pop(0)
                            inst = mod_column(bank[0], wmod_b_sb, kk, ch)
                            if not columns:
                                inst.then_inc(gate_mm, 1)
                    last.then_inc(done, 1)

            pe.wait_ge(consts, 5)
            transpose_xn(0, 0)
            pe.wait_ge(wqkv_hi_done, 3)
            pe.wait_ge(wqkv_lo_done, 3)
            pe.wait_ge(mod_done, 1)
            def project_pair(i):
                transpose_xn(i, 1)
                project(i, 0)
                transpose_xn(i + 1, 0)
                project(i, 1)

            project_pair(0)
            with pe.Fori(1, NI - 1) as i:
                project_pair(i)
            transpose_xn(NI - 1, 1)
            pe.wait_ge(wmod_b_in, 16)
            pe.wait_ge(h_done, NT - 1)
            project(NI - 1, 0, with_columns=True)
            project(NI - 1, 1, with_columns=True)

            def broadcast_gates():
                pe.wait_ge(gate_rep_done, 1)
                for g in range(2 * B):
                    kind, b = divmod(g, B)
                    after(pe, gate_done, g - 1)
                    for f in range(NF):
                        r = ((kind * NF + f) * B + b) * P
                        inst = nc.tensor.transpose(bank[2 + g % 2][:, f * P:(f + 1) * P], gate_rep[:, r:r + P], ident[:, :])
                    inst.then_inc(gate_bc, 1)

            def fill_stack(n, u, q):
                after(pe, stack_done, n + 1)
                if q == 0:
                    after(pe, m_emptied, 2 * n - 1)
                    after(pe, head_out, n - 2)
                else:
                    after(pe, qk_emptied, 4 * n + q)
                if q == 1:
                    after(pe, m_emptied, 2 * n)
                for t in range(4):
                    o = (FILL_ORDER[q] * 4 + t) * P
                    inst = nc.tensor.transpose(turned[:, t * P:(t + 1) * P].bitcast(F32R), stack[u][:, o:o + P],
                                               ident_r[:, :])
                inst.then_inc(qk_filled, 1)

            def score(n, u, j):
                i, k0, width = MAX_PIECES[j]
                after(pe, row_max, NMP * n + j - 1)
                if j == 0:
                    pe.wait_ge(qk_emptied, 4 * n + 2)
                if i == SPLIT_TILES and k0 == 0:
                    pe.wait_ge(qk_emptied, 4 * n + 4)
                diag = k0 + width == (i + 1) * P
                ps = bank[j % 2]
                inst = nc.tensor.matmul(ps[:, 0:width], qk_t[u][:, i * P:(i + 1) * P],
                                        qk_t[u][:, S + k0:S + k0 + width], start=True, stop=not diag)
                if diag:
                    inst = nc.tensor.matmul(ps[:, width - P:width], ident_bf[:, :], mask_bf[:, :], start=False, stop=True)
                inst.then_inc(scores, 1)

            def fill_maxima(n, u, half, ahead=0):
                if half == 0:
                    pe.wait_ge(qk_emptied, 4 * n + 4)
                else:
                    pe.wait_ge(m_emptied, 2 * n + 1)
                    after(pe, head_out, n - 1)
                    if ahead >= 2:
                        pe.wait_ge(qk_emptied, 4 * (n + 1) + 1)
                pe.wait_ge(m_ready, 2 * n + half + 1)
                for t in range(4):
                    c = (u * NI + half * 4 + t) * 2
                    inst = nc.tensor.matmul(turned[0:2, t * P:(t + 1) * P], m_cols[:, c:c + 2], ident_r[:, :],
                                            start=True, stop=True)
                inst.then_inc(m_filled, 1)

            def score_t(n, u, j):
                after(pe, exp_done, NEP * n + j - NTB + 1)
                if j == 0:
                    pe.wait_ge(m_emptied, 2 * n + 1)
                elif j == 2:
                    pe.wait_ge(m_emptied, 2 * n + 2)
                c = 0
                for kt, q0, width in EXP_PIECES[j]:
                    diag = q0 == kt * P
                    inst = nc.tensor.matmul(st_bank[j % NTB][:, c:c + width], qk_t[u][:, S + kt * P:S + (kt + 1) * P],
                                            qk_t[u][:, q0:q0 + width], start=True, stop=not diag)
                    if diag:
                        inst = nc.tensor.matmul(st_bank[j % NTB][:, c:c + P], ident_bf[:, :], mask_t_bf[:, :],
                                                start=False, stop=True)
                    c += width
                inst.then_inc(scores_t, 1)

            def weigh_values(n, u, j, parts, done):
                c = 0
                for kt, q0, width in EXP_PIECES[j]:
                    half, q = divmod(q0, TC)
                    first = parts is probs_hi and width == TC and kt == 0
                    last = parts is probs_lo and (j, kt) == HALF_DONE[half]
                    inst = nc.tensor.matmul(bank[2 + half][0:VH, q:q + width], v_head[u][:, kt * VH:(kt + 1) * VH],
                                            parts[j % NTB][:, c:c + width], start=first, stop=last)
                    c += width
                inst.then_inc(done, 1)

            def weigh_high(n, u, j):
                pe.wait_ge(exp_done, NEP * n + j + 1)
                if j == 0:
                    pe.wait_ge(v_staged, n + 1)
                    after(pe, o_cols_out, 2 * n - 1)
                    if isinstance(n, int) and n == 0:
                        pe.wait_ge(gate_done, 2 * B)
                if j == 2:
                    after(pe, o_cols_out, 2 * n)
                weigh_values(n, u, j, probs_hi, pv_hi_done)

            def weigh_low(n, u, j):
                pe.wait_ge(exp_split, NEP * n + j + 1)
                weigh_values(n, u, j, probs_lo, pv_done)

            def turn_output(n, half, ahead):
                if half == 0:
                    pe.wait_ge(o_cols_out, 2 * (n + 1))
                    after(pe, head_out, n)
                    if ahead >= 1:
                        pe.wait_ge(m_emptied, 2 * (n + 2) + 1)
                for i in range(half * TPC, (half + 1) * TPC):
                    inst = nc.tensor.matmul(turned[:, i * (DH + 1):(i + 1) * (DH + 1)], o_cols[0:VH, i * P:(i + 1) * P],
                                            fold[0:VH, :], start=True, stop=True)
                if half:
                    inst.then_inc(o_turned, 1)

            def unit(n, u, first, ahead):
                for s in range(NEP):
                    late = s >= LATE
                    for stage in (BEFORE, None, AFTER):
                        if stage is None:
                            weigh_high(n, u, s)
                            if s + AHEAD < NEP:
                                score_t(n, u, s + AHEAD)
                            elif ahead >= 1:
                                score_t(n + 1, 1 - u, s + AHEAD - NEP)
                            if s:
                                weigh_low(n, u, s - 1)
                            elif not first:
                                weigh_low(n - 1, 1 - u, NEP - 1)
                            continue
                        for kind, q in stage.get(s, ()):
                            if kind == "fill" and ahead >= 1 + late:
                                fill_stack(*((n + 2, u) if late else (n + 1, 1 - u)), q)
                            if kind == "m" and ahead >= 1:
                                fill_maxima(n + 1, 1 - u, q, ahead)
                            if kind == "turn" and not first:
                                turn_output(n - 1, q, ahead)
                    if ahead >= 1 + late:
                        for j in MAX_AT.get(s, ()):
                            score(*((n + 2, u) if late else (n + 1, 1 - u)), j)

            pe.wait_ge(q_out, NT)
            pe.wait_ge(k_out, NT)
            pe.wait_ge(v_out, NT)
            for q in range(4):
                fill_stack(0, 0, q)
            pe.wait_ge(gate_rep_done, 1)
            for j in range(NMP):
                score(0, 0, j)
            broadcast_gates()
            for half in range(2):
                fill_maxima(0, 0, half)
            for j in range(AHEAD):
                score_t(0, 0, j)
            pe.wait_ge(m_emptied, 2)
            for q in range(3):
                fill_stack(1, 1, q)
            for j in range(4):
                score(1, 1, j)
            for u in range(B):
                unit(u, u, u == 0, 2)
            with pe.Fori(1, H - 1) as h:
                for u in range(B):
                    unit(2 * h + u, u, False, 2)
            for u in range(B):
                unit(2 * (H - 1) + u, u, False, 1 - u)
            weigh_low(UNITS - 1, 1, NEP - 1)
            for half in range(2):
                turn_output(UNITS - 1, half, 0)

            def transpose_o(i, u):
                pe.wait_ge(o_staged, 2 * i + u + 1)
                after(pe, o_lo_done, 2 * i + u - 1)
                for f in range(NF):
                    inst = nc.tensor.transpose(bank[u][:, f * P:(f + 1) * P], o_tile[u][:, f * P:(f + 1) * P], ident[:, :])
                inst.then_inc(o_t, 1)

            def project_out(i, u):
                pe.wait_ge(o_hi_done, 2 * i + u + 1)
                pe.wait_ge(o_lo_done, 2 * i + u + 1)
                after(pe, res_done, 2 * i + u - 1)
                n = 0
                for a, w in ((o_hi, wo_hi), (o_hi, wo_lo), (o_lo, wo_hi)):
                    for f in range(NF):
                        inst = nc.tensor.matmul(bank[2 + u][:, :], a[u][:, f * P:(f + 1) * P], w[u][:, f * D:(f + 1) * D],
                                                start=(n == 0), stop=(n == 3 * NF - 1))
                        n += 1
                inst.then_inc(attn_mm, 1)

            def transpose_xn2(i, u):
                pe.wait_ge(xn_done, NT + 2 * i + u + 1)
                after(pe, h2_done, 2 * i + u - 1)
                for f in range(NF):
                    inst = nc.tensor.transpose(wide[u][:, f * P:(f + 1) * P], xn2[u][:, f * P:(f + 1) * P], ident[:, :])
                inst.then_inc(xn2_t, 1)

            pe.wait_ge(head_out, UNITS)
            for u in range(2):
                transpose_o(0, u)
            pe.wait_ge(wo_ready, 2)
            def project_out_pair(i, first=False, last=False):
                if not last:
                    for u in range(2):
                        transpose_o(i + 1, u)
                for u in range(2):
                    project_out(i, u)
                if not first:
                    for u in range(2):
                        transpose_xn2(i - 1, u)

            project_out_pair(0, first=True)
            project_out_pair(1)
            with pe.Fori(2, NI - 2) as i:
                project_out_pair(i)
            project_out_pair(NI - 2)
            project_out_pair(NI - 1, last=True)
            for u in range(2):
                transpose_xn2(NI - 1, u)

            def gate_up(w, v, c):
                for m in range(NM):
                    for side, (ps, done, read) in enumerate(((wide[0], gate_ps, silu_ps), (wide[1], up_ps, gated))):
                        after(pe, read, NM * (w - 1) + m + 1)
                        n = 0
                        for ww, a in ((w_gu_hi, h2_hi), (w_gu_lo, h2_hi), (w_gu_hi, h2_lo)):
                            for f in range(NF):
                                w0 = (side * NF + f) * HC + m * P
                                a0 = f * B * S + c * TC
                                inst = nc.tensor.matmul(ps[:, m * TC:(m + 1) * TC], ww[v][:, w0:w0 + P], a[:, a0:a0 + TC],
                                                        start=(n == 0), stop=(n == 3 * NF - 1))
                                n += 1
                        inst.then_inc(done, 1)

            def down(w, v, c):
                b, p = c // (NC // B), c % 2
                pe.wait_ge(hid_hi_done, w + 1)
                pe.wait_ge(hid_lo_done, w + 1)
                for t in range(TPC):
                    pe.wait_ge(res_done, NT + TPC * (w - 1) + t + 1)
                    n = 0
                    for a, ww in ((hid_hi, w_dn_hi), (hid_hi, w_dn_lo), (hid_lo, w_dn_hi)):
                        for m in range(NM):
                            inst = nc.tensor.matmul(bank[t][:, :], a[p][:, m * TC + t * P:m * TC + (t + 1) * P],
                                                    ww[v][:, (b * NM + m) * D:(b * NM + m + 1) * D],
                                                    start=(n == 0), stop=(n == 3 * NM - 1))
                            n += 1
                    inst.then_inc(down_ps, 1)

            pe.wait_ge(res_done, NT)
            def slice_pair(jj, last):
                for n in range(2 * NC):
                    w, v, c = jj * 2 * NC + n, n // NC, n % NC
                    if not (last and n == 2 * NC - 1):
                        v1, c1 = (n + 1) // NC % 2, (n + 1) % NC
                        if c1 == 0:
                            pe.wait_ge(w_gu_ready, jj * 2 + v + 2)
                        gate_up(w + 1, v1, c1)
                    if c == 0:
                        pe.wait_ge(w_dn_ready, jj * 2 + v + 1)
                    down(w, v, c)

            pe.wait_ge(w_gu_ready, 1)
            pe.wait_ge(h2_done, NT)
            pe.wait_ge(h2_hi_done, 2 * TPC - 1)
            pe.wait_ge(h2_lo_done, 2 * TPC - 1)
            gate_up(0, 0, 0)
            pe.wait_ge(h2_hi_done, NT)
            pe.wait_ge(h2_lo_done, NT)
            with pe.Fori(0, NJ // 2 - 1) as jj:
                slice_pair(jj, False)
            slice_pair(NJ // 2 - 1, True)

        @block.scalar
        def _(act):
            act.wait_ge(c_in, 16)
            nc.scalar.activation(silu_c[:, :], c_sb[:, :], ACT.Silu).then_inc(silu_done, 1)

            def std_of(u, count):
                act.wait_ge(aggr, count)
                nc.scalar.activation(std[:, u:u + 1], mv[:, 2 * u + 1:2 * u + 2], ACT.Sqrt,
                                     bias=eps_sb[:, 0:1]).then_inc(std_done, 1)

            def modulate(i, u):
                act.wait_ge(xn_t, 2 * i + u + 1)
                after(act, lo_done, 2 * i + u - 1)
                after(act, v_mm, 2 * i + u - 1)
                for f in range(NF):
                    inst = nc.scalar.activation(h1[u][:, f * P:(f + 1) * P], bank[u][:, f * P:(f + 1) * P], ACT.Identity,
                                                bias=mod(SA, f, u), scale=mod(CA, f, u))
                inst.then_inc(h_done, 1)
                act.wait_ge(h_done, 2 * i + u + 1)
                nc.scalar.activation(h1_hi[u][:, :], h1[u][:, :], ACT.Copy).then_inc(hi_done, 1)

            def store_qk(i, u):
                o = (i + u * NI) * DH
                view = qk_raw[:, :].rearrange("p (h w n) -> p h w n", h=H, w=2)
                for which, (mm, done) in enumerate(((q_mm, q_out), (k_mm, k_out))):
                    act.wait_ge(mm, 2 * i + u + 1)
                    nc.scalar.activation(view[:, :, which, bass.ds(o, DH)],
                                         wide[u][:, which * 512:(which + 1) * 512].rearrange("p (h d) -> p h d", d=DH),
                                         ACT.Copy).then_inc(done, 1)

            act.wait_ge(consts, 5)
            std_of(0, 1)
            std_of(1, 2)
            for w in range(3):
                act.wait_ge(wqkv_in[w], 16)
                nc.scalar.activation(wqkv_hi[:, w * NF * D:(w + 1) * NF * D], wqkv_st[:, w * NF * D:(w + 1) * NF * D],
                                     ACT.Copy).then_inc(wqkv_hi_done, 1)
            act.wait_ge(mod_done, 1)
            modulate(0, 0)

            def pair1(i):
                std_of(0, 2 * i + 3)
                modulate(i, 1)
                store_qk(i, 0)
                std_of(1, 2 * i + 4)
                modulate(i + 1, 0)
                store_qk(i, 1)

            pair1(0)
            with act.Fori(1, NI - 1) as i:
                pair1(i)
            modulate(NI - 1, 1)
            store_qk(NI - 1, 0)
            store_qk(NI - 1, 1)

            def empty_stack(n, u, q):
                act.wait_ge(qk_filled, 4 * n + q + 1)
                nc.scalar.activation(qk_t[u][:, FILL_ORDER[q] * TC:(FILL_ORDER[q] + 1) * TC], turned, ACT.Copy
                                     ).then_inc(qk_emptied, 1)

            def empty_maxima(n, u, half):
                act.wait_ge(m_filled, 2 * n + half + 1)
                nc.scalar.activation(qk_t[u][0:2, half * TC:(half + 1) * TC], turned[0:2, :], ACT.Copy
                                     ).then_inc(m_emptied, 1)

            def exponentials(n, j):
                act.wait_ge(scores_t, NEP * n + j + 1)
                after(act, exp_split, NEP * n + j - NTB + 1)
                nc.scalar.activation(probs_t[j % NTB][:, :], st_bank[j % NTB], ACT.Exp)
                after(act, pv_hi_done, NEP * n + j - NTB + 1)
                nc.scalar.activation(probs_hi[j % NTB][:, :], st_bank[j % NTB], ACT.Exp).then_inc(exp_done, 1)

            def empty_output(n, half):
                act.wait_ge(pv_done, NEP * n + HALF_DONE[half][0] + 1)
                after(act, o_turned, n)
                nc.scalar.activation(o_cols[0:VH, half * TC:(half + 1) * TC], bank[2 + half][0:VH, :], ACT.Copy
                                     ).then_inc(o_cols_out, 1)

            def unit(n, u, first, ahead):
                for s in range(NEP):
                    late = s >= LATE
                    if s == EVAC_AT[0]:
                        empty_output(n, 0)
                    if s == EVAC_AT[1] and not first:
                        empty_output(n - 1, 1)
                    for kind, q in BEFORE.get(s, []) + AFTER.get(s, []):
                        if kind == "fill" and ahead >= 1 + late:
                            empty_stack(*((n + 2, u) if late else (n + 1, 1 - u)), q)
                        if kind == "m" and q == 0 and ahead >= 1:
                            empty_maxima(n + 1, 1 - u, 0)
                    if s + AHEAD < NEP:
                        exponentials(n, s + AHEAD)
                    elif ahead >= 1:
                        exponentials(n + 1, s + AHEAD - NEP)

            act.wait_ge(v_out, NT)
            for q in range(4):
                empty_stack(0, 0, q)
            for g in range(2 * B):
                act.wait_ge(gate_bc, g + 1)
                nc.scalar.activation(gates[:, g * D:(g + 1) * D], bank[2 + g % 2][:, :], ACT.Copy).then_inc(gate_done, 1)
            empty_maxima(0, 0, 0)
            for j in range(AHEAD):
                exponentials(0, j)
            for q in range(3):
                empty_stack(1, 1, q)
            for u in range(B):
                unit(u, u, u == 0, 2)
            with act.Fori(1, H - 1) as h:
                for u in range(B):
                    unit(2 * h + u, u, False, 2)
            for u in range(B):
                unit(2 * (H - 1) + u, u, False, 1 - u)
            empty_output(UNITS - 1, 1)

            def high_o(i, u):
                act.wait_ge(o_t, 2 * i + u + 1)
                after(act, attn_mm, 2 * i + u - 1)
                nc.scalar.activation(o_hi[u][:, :], bank[u][:, :], ACT.Copy).then_inc(o_hi_done, 1)

            def modulate2(i, u):
                act.wait_ge(xn2_t, 2 * i + u + 1)
                after(act, h2_lo_done, 2 * i + u - 1)
                for f in range(NF):
                    inst = nc.scalar.activation(h2[u][:, f * P:(f + 1) * P], wide[u][:, f * P:(f + 1) * P], ACT.Identity,
                                                bias=mod(SB, f, u), scale=mod(CB, f, u))
                inst.then_inc(h2_done, 1)
                act.wait_ge(h2_done, 2 * i + u + 1)
                nc.scalar.activation(h2_hi[:, :].rearrange("p (f n) -> p f n", f=NF)[:, :, bass.ds((i + u * NI) * P, P)],
                                     h2[u][:, :].rearrange("p (f n) -> p f n", f=NF), ACT.Copy).then_inc(h2_hi_done, 1)

            act.wait_ge(head_out, UNITS)
            act.wait_ge(wo_ready, 2)
            for u in range(2):
                high_o(0, u)
            def pair3(i, first=False, last=False):
                for u in range(2):
                    if not last:
                        high_o(i + 1, u)
                    std_of(u, NT + 2 * i + u + 1)
                if not first:
                    for u in range(2):
                        modulate2(i - 1, u)

            pair3(0, first=True)
            pair3(1)
            with act.Fori(2, NI - 2) as i:
                pair3(i)
            pair3(NI - 2)
            act.wait_ge(wffn_in, 16)
            nc.scalar.activation(w_gu_hi[0][:, :], wffn_st[:, 0:GU], ACT.Copy).then_inc(gu_split, 1)
            pair3(NI - 1, last=True)
            for u in range(2):
                modulate2(NI - 1, u)

            def unit(w, p):
                for m in range(NM):
                    act.wait_ge(gate_ps, NM * w + m + 1)
                    after(act, hid_lo_done, w)
                    nc.scalar.activation(hidden[:, m * TC:(m + 1) * TC], wide[0][:, m * TC:(m + 1) * TC],
                                         ACT.Silu).then_inc(silu_ps, 1)
                act.wait_ge(gated, NM * (w + 1))
                after(act, down_ps, TPC * (w - 1))
                nc.scalar.activation(hid_hi[p][:, :], hidden[:, :], ACT.Copy).then_inc(hid_hi_done, 1)

            act.wait_ge(o_staged, NT)
            unit(0, 0)
            unit(1, 1)
            with act.Fori(1, NJ * NC // 2) as ww:
                unit(2 * ww, 0)
                unit(2 * ww + 1, 1)

        @block.vector
        def _(dve):
            def moments(src, u, count):
                apart(dve)
                nc.vector.bn_stats(stat6[:, 6 * u:6 * u + 6], src).then_inc(stats, 1)
                dve.wait_ge(stats, count)
                apart(dve)
                nc.vector.bn_aggr(mv[:, 2 * u:2 * u + 2], stat6[:, 6 * u:6 * u + 6]).then_inc(aggr, 1)

            def normalise(src, dst, u, count):
                dve.wait_ge(std_done, count)
                nc.vector.reciprocal(rstd[:, u:u + 1], std[:, u:u + 1]).then_inc(rstd_done, 1)
                dve.wait_ge(rstd_done, count)
                nc.vector.tensor_scalar(dst, src, mv[:, 2 * u:2 * u + 1], rstd[:, u:u + 1], ALU.subtract, ALU.mult
                                        ).then_inc(xn_done, 1)

            def norm1(i, u):
                dve.wait_ge(x_in[u], 16 * (i + 1))
                moments(x_t[u][:, :], u, 2 * i + u + 1)
                after(dve, xn_t, 2 * i + u - 1)
                normalise(x_t[u][:, :], xn1[u][:, :], u, 2 * i + u + 1)

            def store_v(i, u):
                dve.wait_ge(v_mm, 2 * i + u + 1)
                nc.vector.tensor_copy(v_raw[:, :].rearrange("p (h n) -> p h n", h=H)[:, :, bass.ds((i + u * NI) * DH, DH)],
                                      bank[2 + u][:, :].rearrange("p (h d) -> p h d", d=DH)).then_inc(v_out, 1)

            dve.wait_ge(consts, 5)
            norm1(0, 0)
            norm1(0, 1)
            dve.wait_ge(mod_mm, 1)
            one_plus = modcol[:, :].rearrange("p (k n) -> p k n", k=4)
            ps_kinds = bank[3][:, 0:4 * NF * B].rearrange("p (k n) -> p k n", k=4)
            for kind in (SA, CA):
                inst = nc.vector.tensor_scalar(one_plus[:, kind], ps_kinds[:, kind], float(kind in (CA, CB)), None, ALU.add)
            inst.then_inc(mod_done, 1)
            for w in range(3):
                dve.wait_ge(wqkv_hi_done, w + 1)
                seg = slice(w * NF * D, (w + 1) * NF * D)
                nc.vector.tensor_tensor(wqkv_lo[:, seg], wqkv_st[:, seg], wqkv_hi[:, seg].bitcast(F32), ALU.subtract
                                        ).then_inc(wqkv_lo_done, 1)
            with dve.Fori(0, NI - 1) as i:
                norm1(i + 1, 0)
                store_v(i, 0)
                norm1(i + 1, 1)
                store_v(i, 1)
            store_v(NI - 1, 0)
            store_v(NI - 1, 1)

            def make_gates():
                dve.wait_ge(gate_mm, 1)
                for kind in (SB, CB):
                    o = (kind - SB) * NF * B
                    nc.vector.tensor_scalar(one_plus[:, kind], bank[0][:, o:o + NF * B], float(kind == CB), None, ALU.add)
                gps = bank[0][:, 2 * NF * B:4 * NF * B]
                nc.vector.tensor_scalar(gatesgn[:, :], gps, 0.0, 2.0, ALU.is_ge, ALU.mult).then_inc(gate_col, 1)
                dve.wait_ge(gate_col, 1)
                nc.vector.tensor_scalar(gatesgn[:, :], gatesgn[:, :], -1.0, None, ALU.add).then_inc(gate_col, 1)
                dve.wait_ge(gate_col, 2)
                nc.vector.tensor_tensor(gatecol[:, :], gps, gatesgn[:, :], ALU.mult).then_inc(gate_col, 1)
                dve.wait_ge(gate_col, 3)
                nc.vector.tensor_scalar(gatecol[:, :], gatecol[:, :], GATE_MIN, None, ALU.max).then_inc(gate_col, 1)
                dve.wait_ge(gate_col, 4)
                nc.vector.tensor_tensor(gatecol[:, :], gatecol[:, :], gatesgn[:, :], ALU.mult).then_inc(gate_col, 1)
                dve.wait_ge(gate_col, 5)
                nc.vector.tensor_copy(gate_rep[:, :].rearrange("p (g r) -> p g r", r=P),
                                      gatecol[:, :].unsqueeze(2).broadcast_to([P, 2 * NF * B, P])).then_inc(gate_rep_done, 1)

            def maxima(n, u, j):
                i, k0, width = MAX_PIECES[j]
                dst = negmax[:, u * NI + i:u * NI + i + 1]
                if k0:
                    c = u * (NI - SPLIT_TILES) + i - SPLIT_TILES
                    dst = negmax_b[:, c:c + 1]
                dve.wait_ge(scores, NMP * n + j + 1)
                nc.vector.tensor_reduce(dst, bank[j % 2][:, 0:width], AX.X, ALU.max, negate=True).then_inc(row_max, 1)

            def split_probs(n, j):
                dve.wait_ge(exp_done, NEP * n + j + 1)
                after(dve, pv_done, NEP * n + j - NTB + 1)
                nc.vector.tensor_tensor(probs_lo[j % NTB][:, :], probs_t[j % NTB][:, :],
                                        probs_hi[j % NTB][:, :].bitcast(F32), ALU.subtract).then_inc(exp_split, 1)

            def split_maxima(n, u, half):
                dve.wait_ge(row_max, NMP * n + M_PIECES[half])
                t0 = half * SPLIT_TILES
                m = negmax[:, u * NI + t0:u * NI + t0 + SPLIT_TILES]
                parts = m_cols[:, (u * NI + t0) * 2:(u * NI + t0 + SPLIT_TILES) * 2].rearrange("p (t s) -> p t s", s=2)
                if half:
                    nc.vector.tensor_tensor(m, m, negmax_b[:, u * SPLIT_TILES:(u + 1) * SPLIT_TILES], ALU.min
                                            ).then_inc(m_step, 1)
                    dve.wait_ge(m_step, 3 * n + 2)
                after(dve, m_filled, 2 * (n - 1))
                nc.vector.tensor_copy(parts[:, :, 0], m).then_inc(m_step, 1)
                dve.wait_ge(m_step, 3 * n + 1 + 2 * half)
                nc.vector.tensor_tensor(parts[:, :, 1], m, parts[:, :, 0].bitcast(F32), ALU.subtract).then_inc(m_ready, 1)

            def empty_maxima(n, u, half):
                dve.wait_ge(m_filled, 2 * n + half + 1)
                nc.vector.tensor_copy(qk_t[u][0:2, half * TC:(half + 1) * TC], turned[0:2, :]).then_inc(m_emptied, 1)

            def head_output(n, u, h):
                dve.wait_ge(o_turned, n + 1)
                ps = turned[:, 0:NI * (DH + 1)].rearrange("p (i e) -> p i e", e=DH + 1)
                after(dve, head_out, n)
                nc.vector.reciprocal(rinv[:, u * NI:(u + 1) * NI], ps[:, :, DH]).then_inc(rinv_done, 1)
                dve.wait_ge(rinv_done, n + 1)
                dst = o_all[:, u * NI * D:(u + 1) * NI * D].rearrange("p (i n) -> p i n", i=NI)[:, :, bass.ds(h * DH, DH)]
                nc.vector.tensor_tensor(dst, ps[:, :, 0:DH],
                                        rinv[:, u * NI:(u + 1) * NI].unsqueeze(2).broadcast_to([P, NI, DH]), ALU.mult
                                        ).then_inc(head_out, 1)

            def stack_high(n, u):
                dve.wait_ge(roped_done, n + 1)
                after(dve, qk_filled, 4 * (n - 1))
                st = stack[u][:, :].rearrange("p (w t s d) -> p w t s d", w=2, s=4, d=DH)
                src = roped[:, :].rearrange("p (w t d) -> p w t d", w=2, d=DH)
                for w, parts in enumerate((slice(1, 3), slice(1, 4, 2))):
                    inst = nc.vector.tensor_copy(st[:, w, :, parts], src[:, w].unsqueeze(2).broadcast_to([P, NI, 2, DH]))
                inst.then_inc(stack_hi, 1)

            def unit(n, u, h, first, ahead):
                for s in range(NEP):
                    if s == M_AT and ahead >= 1:
                        empty_maxima(n + 1, 1 - u, 1)
                    split_probs(n, s)
                    if s == OUT_AT and not first:
                        head_output(n - 1, 1 - u, h - (1 - u))
                    before = (s - 1) % NEP
                    late = s - 1 >= LATE
                    if ahead >= 1 + late:
                        for j in MAX_AT.get(before, ()):
                            maxima(*((n + 2, u) if late else (n + 1, 1 - u)), j)
                    for half in range(2):
                        if s == SPLIT_AT[half] and ahead >= 1:
                            split_maxima(n + 1, 1 - u, half)
                    if s == HIGH_AT and ahead >= 3:
                        stack_high(n + 3, 1 - u)

            dve.wait_ge(v_mm, NT)
            for u in range(B):
                st = stack[u][:, :].rearrange("p (w t s d) -> p w t s d", w=2, s=4, d=DH)
                for w in range(2):
                    inst = nc.vector.tensor_copy(st[:, w, :, 0],
                                                 part0[:, w * DH:(w + 1) * DH].unsqueeze(1).broadcast_to([P, NI, DH]))
            inst.then_inc(stack_const, 1)
            stack_high(0, 0)
            make_gates()
            stack_high(1, 1)
            for j in range(NMP):
                maxima(0, 0, j)
            for half in range(2):
                split_maxima(0, 0, half)
            empty_maxima(0, 0, 1)
            for j in range(2):
                maxima(1, 1, j)
            stack_high(2, 0)
            for u in range(B):
                unit(u, u, 0, u == 0, 3)
            with dve.Fori(1, H - 2) as h:
                for u in range(B):
                    unit(2 * h + u, u, h, False, 3)
            for n in range(UNITS - 2 * B, UNITS):
                unit(n, n % B, n // B, False, UNITS - 1 - n)
            head_output(UNITS - 1, 1, H - 1)

            def low_o(i, u):
                dve.wait_ge(o_hi_done, 2 * i + u + 1)
                after(dve, attn_mm, 2 * i + u - 1)
                nc.vector.tensor_tensor(o_lo[u][:, :], bank[u][:, :], o_hi[u][:, :].bitcast(F32), ALU.subtract
                                        ).then_inc(o_lo_done, 1)

            def stage_o(i, u):
                after(dve, o_t, 2 * i + u - 1)
                apart(dve)
                nc.vector.tensor_copy(o_tile[u][:, :], o_all[:, bass.ds((i + u * NI) * D, D)]).then_inc(o_staged, 1)

            def residual(i, u):
                tile = x_res[:, bass.ds((i + u * NI) * D, D)]
                dve.wait_ge(attn_mm, 2 * i + u + 1)
                nc.vector.tensor_tensor(tile, bank[2 + u][:, :], tile, ALU.add).then_inc(res_done, 1)

            def norm2(i, u):
                after(dve, xn2_t, 2 * i + u - 1)
                normalise(x_res[:, bass.ds((i + u * NI) * D, D)], xn2[u][:, :], u, NT + 2 * i + u + 1)

            def pair3(i, low=True, stage=True):
                if stage:
                    for u in range(2):
                        stage_o(i + 2, u)
                for u in range(2):
                    residual(i, u)
                    if low:
                        low_o(i + 1, u)
                    dve.wait_ge(res_done, 2 * i + u + 1)
                    moments(x_res[:, bass.ds((i + u * NI) * D, D)], u, NT + 2 * i + u + 1)
                for u in range(2):
                    norm2(i, u)

            dve.wait_ge(head_out, UNITS)
            for u in range(2):
                stage_o(0, u)
            for u in range(2):
                low_o(0, u)
            for u in range(2):
                stage_o(1, u)
            dve.wait_ge(xr_in, 16 * B)
            pair3(0)
            with dve.Fori(1, NI - 2) as i:
                pair3(i)
            pair3(NI - 2, stage=False)
            pair3(NI - 1, low=False, stage=False)
            dve.wait_ge(gu_split, 1)
            nc.vector.tensor_tensor(w_gu_lo[0][:, :], wffn_st[:, 0:GU], w_gu_hi[0][:, :].bitcast(F32), ALU.subtract
                                    ).then_inc(w_gu_ready, 1)

            def gate_hidden(w):
                for m in range(NM):
                    seg = slice(m * TC, (m + 1) * TC)
                    dve.wait_ge(up_ps, NM * w + m + 1)
                    dve.wait_ge(silu_ps, NM * w + m + 1)
                    nc.vector.tensor_tensor(hidden[:, seg], wide[1][:, seg], hidden[:, seg], ALU.mult).then_inc(gated, 1)

            def accumulate(w, c):
                for t in range(TPC):
                    tile = x_res[:, (c * TPC + t) * D:(c * TPC + t + 1) * D]
                    dve.wait_ge(down_ps, TPC * w + t + 1)
                    nc.vector.tensor_tensor(tile, bank[t][:, :], tile, ALU.add).then_inc(res_done, 1)

            def slice_pair(jj, last):
                for n in range(2 * NC):
                    w = jj * 2 * NC + n
                    if not (last and n == 2 * NC - 1):
                        gate_hidden(w + 1)
                    accumulate(w, n % NC)

            gate_hidden(0)
            with dve.Fori(0, NJ // 2 - 1) as jj:
                slice_pair(jj, False)
            slice_pair(NJ // 2 - 1, True)

        @block.gpsimd
        def _(pool):
            pool.memset(ident[:, :], 0.0).then_inc(consts, 1)
            pool.wait_ge(consts, 1)
            pool.affine_select(out=ident[:, :], in_=ident[:, :], compare_op=ALU.not_equal, fill=1.0,
                               base=0, pattern=[[-1, P]], channel_multiplier=1).then_inc(consts, 1)
            pool.memset(eps_sb[:, :], EPS)
            pool.memset(part0[:, :], 0.0)
            pool.memset(ones[:, :], 1.0)
            pool.memset(fold[:, :], 0.0)
            pool.memset(mask_t_bf[:, :], 0.0)
            pool.memset(mask_bf[:, :], 0.0).then_inc(consts, 1)
            pool.wait_ge(consts, 3)
            pool.memset(part0[:, DH:DH + 2], 1.0)
            pool.affine_select(out=fold[:, 0:DH], in_=fold[:, 0:DH], compare_op=ALU.not_equal, fill=1.0,
                               base=0, pattern=[[-1, DH]], channel_multiplier=1).then_inc(consts, 1)
            pool.tensor_copy(ident_bf[:, :], ident[:, :])
            pool.tensor_copy(ident_r[:, :], ident[:, :])
            pool.affine_select(out=mask_t_bf[:, :], in_=mask_t_bf[:, :], compare_op=ALU.is_ge, fill=MASKED,
                               base=0, pattern=[[1, P]], channel_multiplier=-1)
            pool.wait_ge(consts, 4)
            pool.affine_select(out=fold[:, :], in_=fold[:, :], compare_op=ALU.not_equal, fill=1.0,
                               base=-DH, pattern=[[-1, DH + 1]], channel_multiplier=1)
            pool.affine_select(out=mask_bf[:, :], in_=mask_bf[:, :], compare_op=ALU.is_ge, fill=MASKED,
                               base=0, pattern=[[-1, P]], channel_multiplier=1).then_inc(consts, 1)

            def low_h(i, u):
                pool.wait_ge(hi_done, 2 * i + u + 1)
                after(pool, v_mm, 2 * i + u - 1)
                nc.gpsimd.tensor_tensor(h1_lo[u][:, :], h1[u][:, :], h1_hi[u][:, :].bitcast(F32), ALU.subtract
                                        ).then_inc(lo_done, 1)

            for u in range(2):
                low_h(0, u)
            with pool.Fori(1, NI) as i:
                for u in range(2):
                    low_h(i, u)

            def rotate(n, u, h):
                raw = qk_raw[:, bass.ds(h * 2 * NT * DH, 2 * NT * DH)].rearrange(
                    "p (w n) -> p w n", w=2)[:, :, u * NI * DH:(u + 1) * NI * DH]
                raw_pair = raw.rearrange("p w (n two) -> p w n two", two=2)
                tab, pair = "p (w n) -> p w n", "p (w n two) -> p w n two"
                after(pool, roped_done, n)
                pool.tensor_tensor(rope_a[:, :].rearrange(tab, w=2), raw, cos_sb[:, :].rearrange(tab, w=2), ALU.mult)
                for odd in range(2):
                    inst = pool.tensor_tensor(rope_b[:, :].rearrange(pair, w=2, two=2)[:, :, :, odd],
                                              raw_pair[:, :, :, 1 - odd],
                                              sin_sb[:, :].rearrange(pair, w=2, two=2)[:, :, :, odd], ALU.mult)
                inst.then_inc(rope_step, 1)
                pool.wait_ge(rope_step, n + 1)
                after(pool, stack_done, n)
                pool.tensor_tensor(roped[:, :], rope_a[:, :], rope_b[:, :], ALU.add).then_inc(roped_done, 1)

            def stage_v(n, u, h):
                after(pool, pv_done, NEP * (n - 1))
                apart(pool)
                src = v_raw[:, bass.ds(h * NT * DH + u * NI * DH, NI * DH)].rearrange("p (t d) -> p t d", d=DH)
                dst = v_head[u][:, :].rearrange("p (t e) -> p t e", e=VH)
                pool.tensor_copy(dst[:, :, 0:DH], src).then_inc(v_hi_done, 1)
                pool.wait_ge(v_hi_done, n + 1)
                apart(pool)
                pool.tensor_tensor(dst[:, :, DH:2 * DH], src, dst[:, :, 0:DH].bitcast(F32), ALU.subtract
                                   ).then_inc(v_staged, 1)

            def stack_low(n, u):
                pool.wait_ge(stack_hi, n + 1)
                st = stack[u][:, :].rearrange("p (w t s d) -> p w t s d", w=2, s=4, d=DH)
                src = roped[:, :].rearrange("p (w t d) -> p w t d", w=2, d=DH)
                for w, part in enumerate((3, 2)):
                    inst = pool.tensor_tensor(st[:, w, :, part], src[:, w], st[:, w, :, 1].bitcast(F32), ALU.subtract)
                inst.then_inc(stack_done, 1)

            def stage_unit(n, u, h):
                rotate(n, u, h)
                stage_v(n - 1, 1 - u, h - (1 - u))
                stack_low(n, u)

            pool.wait_ge(rope_in, 32)
            pool.wait_ge(xn_t, NT)
            pool.wait_ge(q_out, NT - 1)
            pool.wait_ge(k_out, NT - 1)
            rotate(0, 0, 0)
            pool.wait_ge(q_out, NT)
            pool.wait_ge(k_out, NT)
            pool.wait_ge(v_out, NT)
            for u in range(B):
                pool.tensor_copy(v_head[u][:, :].rearrange("p (t e) -> p t e", e=VH)[:, :, 2 * DH], ones[:, :])
            stack_low(0, 0)
            stage_unit(1, 1, 0)
            with pool.Fori(1, H) as h:
                for u in range(B):
                    stage_unit(2 * h + u, u, h)
            pool.wait_ge(wo_in, 16)
            pool.wait_ge(gate_done, 2 * B)
            for b in range(B):
                g = gates[:, b * D:(b + 1) * D]
                after(pool, wo_ready, b)
                for f in range(NF):
                    seg = slice(f * D, (f + 1) * D)
                    inst = pool.tensor_tensor(wo_gated[:, seg], wo_st[:, seg], g, ALU.mult)
                inst.then_inc(wo_step, 1)
                pool.wait_ge(wo_step, 2 * b + 1)
                pool.tensor_copy(wo_hi[b][:, :], wo_gated[:, :]).then_inc(wo_step, 1)
                pool.wait_ge(wo_step, 2 * b + 2)
                pool.tensor_tensor(wo_lo[b][:, :], wo_gated[:, :], wo_hi[b][:, :].bitcast(F32), ALU.subtract
                                   ).then_inc(wo_ready, 1)
                if b == 0:
                    stage_v(UNITS - 1, 1, H - 1)

            def low_h2(i, u):
                pool.wait_ge(h2_hi_done, 2 * i + u + 1)
                seg = bass.ds((i + u * NI) * P, P)
                hi = h2_hi[:, :].rearrange("p (f n) -> p f n", f=NF)[:, :, seg]
                lo = h2_lo[:, :].rearrange("p (f n) -> p f n", f=NF)[:, :, seg]
                pool.tensor_tensor(lo, h2[u][:, :].rearrange("p (f n) -> p f n", f=NF), hi.bitcast(F32), ALU.subtract
                                   ).then_inc(h2_lo_done, 1)

            def stage_slice(j, v, part):
                gu = wffn_st[:, 0:GU]
                if part == 0:
                    pool.wait_ge(wffn_in, 16 * (j + 1))
                    after(pool, down_ps, (j - 1) * NC * TPC)
                    apart(pool)
                    pool.tensor_copy(w_gu_hi[v][:, :], gu).then_inc(gu_split, 1)
                elif part == 1:
                    pool.wait_ge(gu_split, j + 1)
                    pool.tensor_tensor(w_gu_lo[v][:, :], gu, w_gu_hi[v][:, :].bitcast(F32), ALU.subtract
                                       ).then_inc(w_gu_ready, 1)
                else:
                    b = part - 2
                    g = gates[:, (B + b) * D:(B + b + 1) * D]
                    seg = slice(b * DN, (b + 1) * DN)
                    if b == 1:
                        pool.wait_ge(dn_ready_0, j + 1)
                    multiplied, split = ((dn_mul, dn_ready_0), (wffn_read, w_dn_ready))[b]
                    for m in range(NM):
                        inst = pool.tensor_tensor(dn_gated[:, m * D:(m + 1) * D],
                                                  wffn_st[:, GU + m * D:GU + (m + 1) * D], g, ALU.mult)
                    inst.then_inc(multiplied, 1)
                    pool.wait_ge(multiplied, j + 1)
                    apart(pool)
                    pool.tensor_copy(w_dn_hi[v][:, seg], dn_gated[:, :]).then_inc(dn_split, 1)
                    pool.wait_ge(dn_split, 2 * j + b + 1)
                    pool.tensor_tensor(w_dn_lo[v][:, seg], dn_gated[:, :], w_dn_hi[v][:, seg].bitcast(F32), ALU.subtract
                                       ).then_inc(split, 1)

            def low_hidden(w, p):
                pool.wait_ge(hid_hi_done, w + 1)
                after(pool, down_ps, TPC * (w - 1))
                pool.tensor_tensor(hid_lo[p][:, :], hidden[:, :], hid_hi[p][:, :].bitcast(F32), ALU.subtract
                                   ).then_inc(hid_lo_done, 1)

            def slice_units(j, stage_v):
                for c in range(NC):
                    low_hidden(j * NC + c, c % 2)
                    if stage_v is not None:
                        stage_slice(j + 1, stage_v, c)

            with pool.Fori(0, NI) as i:
                for u in range(2):
                    low_h2(i, u)
            pool.wait_ge(xn2_t, NT)
            pool.wait_ge(attn_mm, NT)
            pool.wait_ge(h2_lo_done, NT)
            for part in range(2, 4):
                stage_slice(0, 0, part)
            slice_units(0, 1)
            with pool.Fori(0, NJ // 2 - 1) as jj:
                slice_units(2 * jj + 1, 0)
                slice_units(2 * jj + 2, 1)
            slice_units(NJ - 1, None)


def kernel(L0_attn_x, L0_attn_wq, L0_attn_wk, L0_attn_wv, L0_attn_wo, L0_ffn_w_gate, L0_ffn_w_up, L0_ffn_w_down,
           L0_c, L0_wmod):
    import concourse.bacc as _bacc
    from concourse.bass_utils import run_bass_kernel_spmd as _run

    def rows(w):
        w = np.asarray(w)
        return w.reshape(w.shape[0] // P, P, w.shape[1]).transpose(1, 0, 2)

    wq, wk, wv, wo = (rows(np.asarray(w).T) for w in (L0_attn_wq, L0_attn_wk, L0_attn_wv, L0_attn_wo))
    wmod = np.asarray(L0_wmod).reshape(NF, P, 6, D).transpose(1, 2, 0, 3)
    sides = [np.asarray(w).T.reshape(NF, P, NJ, HC).transpose(2, 1, 0, 3).reshape(NJ, P, NF * HC)
             for w in (L0_ffn_w_gate, L0_ffn_w_up)]
    down = np.asarray(L0_ffn_w_down).T.reshape(NJ, NM, P, D).transpose(0, 2, 1, 3).reshape(NJ, P, NM * D)

    inv_freq = np.float32(10000.0) ** (np.float32(-2.0) * np.arange(DH // 2, dtype=np.float32) / np.float32(DH))
    ang = (np.arange(S, dtype=np.float32)[:, None] * inv_freq[None, :]).astype(np.float32)
    scale = np.array([1.0 / np.sqrt(np.float32(DH)), 1.0], np.float32)
    sign = np.tile(np.array([-1.0, 1.0], np.float32), DH // 2)

    def table(t, s):
        t = (np.repeat(t, 2, axis=-1) * s).astype(np.float32)
        t = scale[:, None, None] * t[None]
        return t.reshape(2, NI, P, DH).transpose(2, 0, 1, 3).reshape(P, 2 * NI * DH)

    arrays = {
        "x": np.asarray(L0_attn_x).reshape(B * S, D),
        "c_t": np.asarray(L0_c).T.reshape(NF, P, B).transpose(1, 0, 2).reshape(P, NF * B),
        "wmod_a": wmod[:, [0, 1]].reshape(P, -1),
        "wmod_b": wmod[:, [3, 4, 2, 5]].reshape(P, -1),
        "wqkv": np.stack([wq, wk, wv], 1).reshape(P, -1),
        "wo": wo.reshape(P, -1),
        "wffn": np.concatenate([*sides, down], axis=2).reshape(NJ * P, -1),
        "cos": table(np.cos(ang), 1.0),
        "sin": table(np.sin(ang), sign),
    }
    arrays = {f"{k}_dram": np.ascontiguousarray(v) for k, v in arrays.items()}
    nc = _bacc.Bacc("TRN2", target_bir_lowering=False, num_devices=1)
    args = [nc.dram_tensor(k, v.shape, F32, kind="ExternalInput").ap() for k, v in arrays.items()]
    out = nc.dram_tensor("out_dram", (B * S, D), F32, kind="ExternalOutput").ap()
    adaln_block(nc, *args, out)
    r = _run(nc, [arrays], core_ids=[0])
    return r.results[0]["out_dram"].reshape(B, S, D)
```
